# Optimizing a Trainium2 kernel written in Bass

```python
import numpy as np
import jax
import jax.numpy as jnp

def _softmax(x, axis=-1):
    return jax.nn.softmax(x, axis=axis)

def _gelu(x):
    return jax.nn.gelu(x, approximate=True)

def _silu(x):
    return jax.nn.silu(x)

def _sigmoid(x):
    return jax.nn.sigmoid(x)

def _layernorm(x, axis=-1, eps=1e-05):
    m = jnp.mean(x, axis=axis, keepdims=True)
    v = jnp.var(x, axis=axis, keepdims=True)
    return (x - m) / jnp.sqrt(v + eps)

def _scatter_add(tgt, idx, src, axis=0):
    return tgt.at[idx].add(src)

def _segment_sum(src, seg, n):
    return jax.ops.segment_sum(src, seg, n)
kernel_name = 'mk_adaln_ffn_d2_seqx_r8_25479d'

def setup_inputs(seed: int=0):
    np.random.seed(seed)
    _w = jnp.asarray

    def _rec_inputs():
        import jax
        import jax.numpy as jnp
        _rk = jax.random.key(seed)
        x = -0.000125 + 0.9999 * jax.random.normal(jax.random.fold_in(_rk, 1), (8, 128, 128), jnp.float32)
        _lenS = 128 - jax.random.randint(jax.random.fold_in(_rk, 7), (8,), 0, max(1, 128 // 4) + 1, jnp.int32)
        _lenS2 = 128 - jax.random.randint(jax.random.fold_in(_rk, 8), (8,), 0, max(1, 128 // 4) + 1, jnp.int32)
        cond_512 = 0.00782532 + 1.00527 * jax.random.normal(jax.random.fold_in(_rk, 11), (8, 64), jnp.float32)
        return (x, cond_512)
    x, cond_512 = _rec_inputs()

    def _L0_cond_setup():
        import jax, jax.numpy as jnp
        import numpy as np
        IN_DIM = 128
        OUT_DIM = 128
        MU_DIM = 64
        K = 30
        key = jax.random.key(seed)
        k1, k2, k3, k4, k5 = jax.random.split(key, 5)
        B, S = (16, 256)
        x = jax.random.normal(k1, (B, S, IN_DIM), dtype=jnp.float32)
        mu = jax.random.normal(k2, (B, MU_DIM), dtype=jnp.float32)
        W_dec = jax.random.normal(k3, (MU_DIM, (IN_DIM + 1) * K), dtype=jnp.float32) / np.sqrt(MU_DIM)
        b_dec = jax.random.normal(k4, ((IN_DIM + 1) * K,), dtype=jnp.float32) * 0.01
        V = jax.random.normal(k5, (K, OUT_DIM), dtype=jnp.float32) / np.sqrt(K)
        return {'x': x, 'mu': mu, 'W_dec': W_dec, 'b_dec': b_dec, 'V': V}
    _L0_cond_all = _L0_cond_setup()
    _L0_cond_in = {k: v for k, v in _L0_cond_all.items() if k in ('W_dec', 'b_dec', 'V')}
    del _L0_cond_all

    def _L0_ffn_setup():
        import jax, jax.numpy as jnp
        import numpy as np
        import math
        D = 128
        H = 16
        E = 8
        TOPK = 2
        LAT = D // 2
        KPH = LAT // H
        HD = D // H

        def _forward(hs, q_w, q_b, k_w, k_b, v_w, v_b, o_w, o_b, router_w, router_b, w1, b1, w2, b2):
            B, S, _ = hs.shape
            Q = (hs @ q_w + q_b).reshape(B, S, H, HD).transpose(0, 2, 1, 3)
            K = (hs @ k_w + k_b).reshape(B, S, H, KPH).transpose(0, 2, 1, 3)
            V = (hs @ v_w + v_b).reshape(B, S, H, KPH).transpose(0, 2, 1, 3)
            scores = jnp.einsum('bhsk,bhtk->bhst', Q[..., :KPH], K) / math.sqrt(KPH)
            attn = jax.nn.softmax(scores, axis=-1)
            ao = jnp.einsum('bhst,bhtv->bhsv', attn, V)
            ao = ao.transpose(0, 2, 1, 3).reshape(B, S, H * KPH)
            ao = jnp.concatenate([ao, jnp.zeros((B, S, D - LAT), ao.dtype)], axis=-1)
            mla_out = ao @ o_w + o_b
            probs = jax.nn.softmax(mla_out @ router_w + router_b, axis=-1)
            topw, topi = jax.lax.top_k(probs, TOPK)
            topw = topw / (topw.sum(-1, keepdims=True) + 1e-08)
            combine = jnp.sum(jax.nn.one_hot(topi, E, dtype=probs.dtype) * topw[..., None], axis=-2)
            h1 = jnp.einsum('bsd,edf->ebsf', mla_out, w1) + b1[:, None, None, :]
            h1 = jax.nn.gelu(h1, approximate=False)
            h2 = jnp.einsum('ebsf,efd->ebsd', h1, w2) + b2[:, None, None, :]
            moe_out = jnp.einsum('bse,ebsd->bsd', combine, h2)
            return hs + 0.3 * moe_out
        key = jax.random.key(seed)
        ks = jax.random.split(key, 16)
        s = 0.02
        inp = {'hidden_states': jax.random.normal(ks[0], (2, 256, D), jnp.float32), 'q_w': jax.random.normal(ks[1], (D, D), jnp.float32) * s, 'q_b': jnp.zeros((D,), jnp.float32), 'k_w': jax.random.normal(ks[2], (D, LAT), jnp.float32) * s, 'k_b': jnp.zeros((LAT,), jnp.float32), 'v_w': jax.random.normal(ks[3], (D, LAT), jnp.float32) * s, 'v_b': jnp.zeros((LAT,), jnp.float32), 'o_w': jax.random.normal(ks[4], (D, D), jnp.float32) * s, 'o_b': jnp.zeros((D,), jnp.float32), 'router_w': jax.random.normal(ks[5], (D, E), jnp.float32) * s, 'router_b': jnp.zeros((E,), jnp.float32), 'w1': jax.random.normal(ks[6], (E, D, 2 * D), jnp.float32) * s, 'b1': jnp.zeros((E, 2 * D), jnp.float32), 'w2': jax.random.normal(ks[7], (E, 2 * D, D), jnp.float32) * s, 'b2': jnp.zeros((E, D), jnp.float32)}
        return inp
    _L0_ffn_all = _L0_ffn_setup()
    _L0_ffn_in = {k: v for k, v in _L0_ffn_all.items() if k in ('q_w', 'q_b', 'k_w', 'k_b', 'v_w', 'v_b', 'o_w', 'o_b', 'router_w', 'router_b', 'w1', 'b1', 'w2', 'b2')}
    del _L0_ffn_all

    def _L1_cond_setup():
        import jax, jax.numpy as jnp
        import numpy as np
        import math
        HEAD_NUM = 16
        EPS = 1e-08

        def modulated_linear(x, s, aff_w, aff_b, w, b):
            style = s @ aff_w.T + aff_b
            w_mod = w[None, :, :] * style[:, None, :]
            demod = jax.lax.rsqrt(jnp.sum(w_mod * w_mod, axis=2) + EPS)
            w_mod = w_mod * demod[:, :, None]
            return jnp.einsum('bni,boi->bno', x, w_mod) + b
        key = jax.random.key(seed)
        ks = jax.random.split(key, 6)
        B, N, F, S = (8, 128, 128, 64)
        return {'x': jax.random.normal(ks[0], (B, N, F), dtype=jnp.float32), 's': jax.random.normal(ks[1], (B, S), dtype=jnp.float32), 'k_aff_w': jax.random.normal(ks[2], (F, S), dtype=jnp.float32) * 0.02, 'k_aff_b': jnp.ones((F,), dtype=jnp.float32), 'k_w': jax.random.normal(ks[3], (F, F), dtype=jnp.float32) * 0.02, 'k_b': jnp.zeros((F,), dtype=jnp.float32), 'o_aff_w': jax.random.normal(ks[4], (F, S), dtype=jnp.float32) * 0.02, 'o_aff_b': jnp.ones((F,), dtype=jnp.float32), 'o_w': jax.random.normal(ks[5], (F, F), dtype=jnp.float32) * 0.02, 'o_b': jnp.zeros((F,), dtype=jnp.float32)}
    _L1_cond_all = _L1_cond_setup()
    _L1_cond_in = {k: v for k, v in _L1_cond_all.items() if k in ('k_aff_w', 'k_aff_b', 'k_w', 'k_b', 'o_aff_w', 'o_aff_b', 'o_w', 'o_b')}
    del _L1_cond_all

    def _L1_ffn_setup():
        import jax, jax.numpy as jnp
        import numpy as np
        N_EXPERTS = 8
        TOP_K = 2
        key = jax.random.key(seed)
        k1, k2, k3, k4 = jax.random.split(key, 4)
        B, T, C, H, E = (2, 256, 128, 512, N_EXPERTS)
        x = jax.random.normal(k1, (B, T, C), dtype=jnp.float32)
        router_w = jax.random.normal(k2, (E, C), dtype=jnp.float32) * 0.02
        w1 = jax.random.normal(k3, (E, C, H), dtype=jnp.float32) * (1.0 / np.sqrt(C))
        w2 = jax.random.normal(k4, (E, H, C), dtype=jnp.float32) * (1.0 / np.sqrt(H))
        return {'x': x, 'router_w': router_w, 'w1': w1, 'w2': w2}
    _L1_ffn_all = _L1_ffn_setup()
    _L1_ffn_in = {k: v for k, v in _L1_ffn_all.items() if k in ('router_w', 'w1', 'w2')}
    del _L1_ffn_all
    return {'x': x, 'cond_512': cond_512, 'L0_cond_W_dec': _L0_cond_in['W_dec'], 'L0_cond_b_dec': _L0_cond_in['b_dec'], 'L0_cond_V': _L0_cond_in['V'], 'L0_ffn_q_w': _L0_ffn_in['q_w'], 'L0_ffn_q_b': _L0_ffn_in['q_b'], 'L0_ffn_k_w': _L0_ffn_in['k_w'], 'L0_ffn_k_b': _L0_ffn_in['k_b'], 'L0_ffn_v_w': _L0_ffn_in['v_w'], 'L0_ffn_v_b': _L0_ffn_in['v_b'], 'L0_ffn_o_w': _L0_ffn_in['o_w'], 'L0_ffn_o_b': _L0_ffn_in['o_b'], 'L0_ffn_router_w': _L0_ffn_in['router_w'], 'L0_ffn_router_b': _L0_ffn_in['router_b'], 'L0_ffn_w1': _L0_ffn_in['w1'], 'L0_ffn_b1': _L0_ffn_in['b1'], 'L0_ffn_w2': _L0_ffn_in['w2'], 'L0_ffn_b2': _L0_ffn_in['b2'], 'L1_cond_k_aff_w': _L1_cond_in['k_aff_w'], 'L1_cond_k_aff_b': _L1_cond_in['k_aff_b'], 'L1_cond_k_w': _L1_cond_in['k_w'], 'L1_cond_k_b': _L1_cond_in['k_b'], 'L1_cond_o_aff_w': _L1_cond_in['o_aff_w'], 'L1_cond_o_aff_b': _L1_cond_in['o_aff_b'], 'L1_cond_o_w': _L1_cond_in['o_w'], 'L1_cond_o_b': _L1_cond_in['o_b'], 'L1_ffn_router_w': _L1_ffn_in['router_w'], 'L1_ffn_w1': _L1_ffn_in['w1'], 'L1_ffn_w2': _L1_ffn_in['w2']}

def reference(x, cond_512, L0_cond_W_dec, L0_cond_b_dec, L0_cond_V, L0_ffn_q_w, L0_ffn_q_b, L0_ffn_k_w, L0_ffn_k_b, L0_ffn_v_w, L0_ffn_v_b, L0_ffn_o_w, L0_ffn_o_b, L0_ffn_router_w, L0_ffn_router_b, L0_ffn_w1, L0_ffn_b1, L0_ffn_w2, L0_ffn_b2, L1_cond_k_aff_w, L1_cond_k_aff_b, L1_cond_k_w, L1_cond_k_b, L1_cond_o_aff_w, L1_cond_o_aff_b, L1_cond_o_w, L1_cond_o_b, L1_ffn_router_w, L1_ffn_w1, L1_ffn_w2):
    import jax
    import jax.numpy as jnp

    def _L0_cond_ref(x, mu, W_dec, b_dec, V):
        import jax, jax.numpy as jnp
        import numpy as np
        IN_DIM = 128
        OUT_DIM = 128
        MU_DIM = 64
        K = 30
        B = mu.shape[0]
        U = (mu @ W_dec + b_dec).reshape(B, IN_DIM + 1, K)
        param = jnp.einsum('bik,kj->bij', U, V)
        weight = param[:, :-1, :]
        bias = param[:, -1, :]
        out = jnp.einsum('bsd,bde->bse', x, weight)
        out = out + bias[:, None, :]
        return out

    def _L0_ffn_ref(hidden_states, q_w, q_b, k_w, k_b, v_w, v_b, o_w, o_b, router_w, router_b, w1, b1, w2, b2):
        import jax, jax.numpy as jnp
        import numpy as np
        import math
        D = 128
        H = 16
        E = 8
        TOPK = 2
        LAT = D // 2
        KPH = LAT // H
        HD = D // H

        def _forward(hs, q_w, q_b, k_w, k_b, v_w, v_b, o_w, o_b, router_w, router_b, w1, b1, w2, b2):
            B, S, _ = hs.shape
            Q = (hs @ q_w + q_b).reshape(B, S, H, HD).transpose(0, 2, 1, 3)
            K = (hs @ k_w + k_b).reshape(B, S, H, KPH).transpose(0, 2, 1, 3)
            V = (hs @ v_w + v_b).reshape(B, S, H, KPH).transpose(0, 2, 1, 3)
            scores = jnp.einsum('bhsk,bhtk->bhst', Q[..., :KPH], K) / math.sqrt(KPH)
            attn = jax.nn.softmax(scores, axis=-1)
            ao = jnp.einsum('bhst,bhtv->bhsv', attn, V)
            ao = ao.transpose(0, 2, 1, 3).reshape(B, S, H * KPH)
            ao = jnp.concatenate([ao, jnp.zeros((B, S, D - LAT), ao.dtype)], axis=-1)
            mla_out = ao @ o_w + o_b
            probs = jax.nn.softmax(mla_out @ router_w + router_b, axis=-1)
            topw, topi = jax.lax.top_k(probs, TOPK)
            topw = topw / (topw.sum(-1, keepdims=True) + 1e-08)
            combine = jnp.sum(jax.nn.one_hot(topi, E, dtype=probs.dtype) * topw[..., None], axis=-2)
            h1 = jnp.einsum('bsd,edf->ebsf', mla_out, w1) + b1[:, None, None, :]
            h1 = jax.nn.gelu(h1, approximate=False)
            h2 = jnp.einsum('ebsf,efd->ebsd', h1, w2) + b2[:, None, None, :]
            moe_out = jnp.einsum('bse,ebsd->bsd', combine, h2)
            return hs + 0.3 * moe_out
        return _forward(hidden_states, q_w, q_b, k_w, k_b, v_w, v_b, o_w, o_b, router_w, router_b, w1, b1, w2, b2)

    def _L1_cond_ref(x, s, k_aff_w, k_aff_b, k_w, k_b, o_aff_w, o_aff_b, o_w, o_b):
        import jax, jax.numpy as jnp
        import numpy as np
        import math
        HEAD_NUM = 16
        EPS = 1e-08

        def modulated_linear(x, s, aff_w, aff_b, w, b):
            style = s @ aff_w.T + aff_b
            w_mod = w[None, :, :] * style[:, None, :]
            demod = jax.lax.rsqrt(jnp.sum(w_mod * w_mod, axis=2) + EPS)
            w_mod = w_mod * demod[:, :, None]
            return jnp.einsum('bni,boi->bno', x, w_mod) + b
        B, N, F = x.shape
        H = HEAD_NUM
        D = F // H
        kx = modulated_linear(x, s, k_aff_w, k_aff_b, k_w, k_b)
        kx = kx.reshape(B, N, H, D)
        q = k = v = kx
        scores = jnp.einsum('bnhd,bnjd->bnhj', q, k) / math.sqrt(D)
        A = jax.nn.softmax(scores, axis=-1)
        out = jnp.einsum('bnhj,bnjd->bnhd', A, v).reshape(B, N, F)
        out = modulated_linear(out, s, o_aff_w, o_aff_b, o_w, o_b)
        return out

    def _L1_ffn_ref(x, router_w, w1, w2):
        import jax, jax.numpy as jnp
        import numpy as np
        N_EXPERTS = 8
        TOP_K = 2
        B, T, C = x.shape
        E = N_EXPERTS
        xf = x.reshape(-1, C)
        logits = jnp.einsum('nc,ec->ne', xf, router_w)
        probs = jax.nn.softmax(logits, axis=-1)
        top_w, top_i = jax.lax.top_k(probs, TOP_K)
        top_w = top_w / jnp.sum(top_w, axis=-1, keepdims=True)
        comb = jnp.einsum('nk,nke->ne', top_w, jax.nn.one_hot(top_i, E, dtype=xf.dtype))
        h = jax.nn.gelu(jnp.einsum('nc,ech->enh', xf, w1), approximate=False)
        y = jnp.einsum('enh,ehc->enc', h, w2)
        out = jnp.einsum('ne,enc->nc', comb, y)
        return out.reshape(B, T, C)
    x = x + _L0_ffn_ref(_L0_cond_ref(x, cond_512, L0_cond_W_dec, L0_cond_b_dec, L0_cond_V), L0_ffn_q_w, L0_ffn_q_b, L0_ffn_k_w, L0_ffn_k_b, L0_ffn_v_w, L0_ffn_v_b, L0_ffn_o_w, L0_ffn_o_b, L0_ffn_router_w, L0_ffn_router_b, L0_ffn_w1, L0_ffn_b1, L0_ffn_w2, L0_ffn_b2)
    x = x + _L1_ffn_ref(_L1_cond_ref(x, cond_512, L1_cond_k_aff_w, L1_cond_k_aff_b, L1_cond_k_w, L1_cond_k_b, L1_cond_o_aff_w, L1_cond_o_aff_b, L1_cond_o_w, L1_cond_o_b), L1_ffn_router_w, L1_ffn_w1, L1_ffn_w2)
    return x

_drawn_inputs = setup_inputs


def setup_inputs(seed=0):
    import zlib

    import numpy as np

    out = dict(_drawn_inputs(seed))
    spreads = {'L0_ffn_q_b': (0.0, 0.665),
     'L0_ffn_k_b': (0.0, 2.0),
     'L0_ffn_v_b': (0.0, 0.667),
     'L0_ffn_o_b': (0.0, 0.8),
     'L0_ffn_router_b': (0.0, 0.605),
     'L0_ffn_b1': (0.0, 0.8),
     'L0_ffn_b2': (0.0, 0.8),
     'L1_cond_k_aff_b': (1.0, 0.2),
     'L1_cond_k_b': (0.0, 0.1),
     'L1_cond_o_aff_b': (1.0, 0.2),
     'L1_cond_o_b': (0.0, 1.311)}
    factors = {'L0_ffn_q_w': 4.48,
     'L0_ffn_k_w': 4.284,
     'L0_ffn_v_w': 7.822,
     'L0_ffn_o_w': 7.91,
     'L0_ffn_router_w': 5.182,
     'L0_ffn_w1': 8.0,
     'L0_ffn_w2': 4.87}
    for name, (base, spread) in spreads.items():
        noise = np.random.default_rng([zlib.crc32(name.encode()), seed]).standard_normal(out[name].shape)
        drawn = base * np.exp(spread * noise) if base else spread * noise
        out[name] = jnp.asarray(drawn.astype(out[name].dtype))
    for name, factor in factors.items():
        out[name] = (out[name] * factor).astype(out[name].dtype)
    return out
```

```python
from contextlib import ExitStack

import concourse.bass as bass
from concourse import mybir

BATCH, SEQ, D = 8, 128, 128
TOK = BATCH * SEQ
HALF = 512
HALVES = TOK // HALF
PER_HALF = HALF // SEQ
COND = 64
RANK = 30
HEADS, KPH = 16, 4
GROUPS = HEADS // 4
E = 8
CHUNKS = (256 // 128, 512 // 128)
H1, D1 = 16, D // 16
NEAR = H1 // 2 + 1
MOE_SCALE = 0.3
DEMOD_EPS = 1e-8
TOP_EPS = 1e-8

F32 = mybir.dt.float32
FR = mybir.dt.float32r
F16 = mybir.dt.float16
ALU = mybir.AluOpType
ACT = mybir.ActivationFunctionType
AX = mybir.AxisListType


def columns(*fields):
    at, found = 0, {}
    for name, width in fields:
        found[name] = (at, at + width)
        at += width
    return found, at


COND_AT, COND_W = columns(("wdec", RANK * D), ("ubias", 128), ("cond", BATCH), ("kaff", D), ("oaff", D))
PROJ_AT, PROJ_W = columns(("vt", 128), ("w", 3 * 512))
CONST_AT, CONST_W = columns(
    ("vrep", 128), ("ident", 128), ("wk", D), ("wo", D), ("kb", D), ("ow", GROUPS * D), ("rw0", E), ("rw1", E),
    ("rb", PER_HALF * E), ("rank", PER_HALF * E), ("b1", E * CHUNKS[0]), ("ob0", 1), ("ob1", 1), ("mq", 1), ("mk", 1))

JOBS = [(layer, e, half) for layer in range(2) for e in range(E) for half in range(HALVES)]
CHUNK_LIST = [(j, fc) for j, (layer, _, _) in enumerate(JOBS) for fc in range(CHUNKS[layer])]
FIRST_CHUNK = {j: c for c, (j, fc) in enumerate(CHUNK_LIST) if fc == 0}
END_CHUNK = {j: c + 1 for c, (j, fc) in enumerate(CHUNK_LIST)}
JOBS_PER_LAYER = E * HALVES
LAG = 2


def program(nc, cond_pack, proj_pack, proj_bias, x_t, const_pack, sel_pack, w_layer0, w_layer1, out):
    with ExitStack() as ctx:
        def sb(name, shape, dt=F32):
            return ctx.enter_context(nc.sbuf_tensor(name, shape, dt))

        def sem(name):
            return ctx.enter_context(nc.semaphore(name))

        bank = [ctx.enter_context(nc.psum_tensor(f"bank{i}", [128, 512], F32)) for i in range(8)]

        early = sb("early", [128, COND_W])
        condp = early[0:COND + 1, :]
        ao = early[:, 0:GROUPS * TOK].rearrange("p (g n) -> p g n", g=GROUPS)
        early2 = sb("early2", [128, PROJ_W + 3 * 512])
        projp, projb = early2[:, 0:PROJ_W], early2[:, PROJ_W:]
        g = early2[:, 0:3 * 512].rearrange("p (i n) -> p i n", i=3)
        cbs = early2[:, 3 * 512:5 * 512].rearrange("p (i n) -> p i n", i=2)
        xT = sb("xT", [128, TOK])
        const = sb("const", [128, CONST_W])
        selp = sb("selp", [16, E * 128 + 128])
        raw = sb("raw", [128, 2, 1024])

        def C(name):
            a, b = CONST_AT[name]
            return const[:, a:b]

        def CP(name):
            a, b = COND_AT[name]
            return condp[:, a:b]

        ones32 = sb("ones32", [128, 32])
        eps = sb("eps", [128, 1])
        ident16 = sb("ident16", [128, 128], F16)
        sel = sb("sel", [16, E * 128], FR)
        urep = sb("urep", [128, BATCH, 4, 32])
        ubias = sb("ubias", [128, 8])
        wfull = sb("wfull", [128, 512])
        wst = sb("wst", [128, 3, 512], FR)
        vst = sb("vst", [128, 128], FR)
        ts = sb("ts", [128, TOK], FR)
        hi16 = sb("hi16", [128, 2, 512], F16)
        kop = sb("kop", [128, GROUPS, TOK], F16)
        val = sb("val", [128, BATCH, 512])
        qop = sb("qop", [128, 2, 512], F16)
        negm = sb("negm", [128, 2, GROUPS, 128], F16)
        probs = sb("probs", [128, 2, 4, 512])
        rz = sb("rz", [128, 512])
        xhs = sb("xhs", [128, TOK])
        mo = sb("mo", [128, TOK])
        mo_hi = sb("mo_hi", [128, TOK], FR)
        mo_lo = sb("mo_lo", [128, TOK], FR)
        w_hi = sb("w_hi", [128, 3, 1024], FR)
        w_lo = sb("w_lo", [128, 3, 1024], FR)
        g_hi = sb("g_hi", [128, 3, 512], FR)
        g_lo = sb("g_lo", [128, 3, 512], FR)
        weighted = sb("weighted", [128, 2, 512])
        acc = xT
        x1 = sb("x1", [128, TOK])
        rt = sb("rt", [128, 8, PER_HALF, E])
        rs = sb("rs", [128, 8, PER_HALF, 1])
        parts = sb("parts", [128, PER_HALF, 2 * E], FR)
        comb_t = sb("comb_t", [16, HALVES, HALF], FR)
        style = sb("style", [128, 2, BATCH])
        style2 = sb("style2", [128, 2, BATCH])
        wsq = sb("wsq", [128, 2, D])
        wmod = sb("wmod", [128, 2, BATCH, D])
        demod = probs[:, 0:2, 0:2, :].rearrange("p w a b -> p w (a b)")
        kx2 = val[:, 0, :].rearrange("p (i c) -> p i c", i=2)
        dots = val[:, 1:4, :].rearrange("p a b -> p (a b)")[:, 0:NEAR * D]
        gram = val[:, 4:6, :].rearrange("p i (s h) -> p i s h", s=16)
        amat = val[:, 6, :].rearrange("p (i s h) -> p i s h", i=2, s=H1)
        att_t = val[:, 7, 0:256].rearrange("p (i c) -> p i c", i=2)
        prod = probs[:, :, :, :].rearrange("p i a b -> p i (a b)")
        small = sb("small", [128, 2, 2, H1])

        def view(t, first, dims):
            a = t[:, ...] if not isinstance(t, bass.AP) else t
            return bass.AP(tensor=a.tensor, offset=a.offset + first, ap=[list(a.ap[0]), *[list(x) for x in dims]])

        ld_proj, ld_cond, ld_const = sem("ld_proj"), sem("ld_cond"), sem("ld_const")
        ld_w = [sem("ld_w_even"), sem("ld_w_odd")]
        stored = sem("stored")
        consts_made = sem("consts_made")
        wstack_mm, wstack_done = sem("wstack_mm"), sem("wstack_done")
        u_mm, u_done = sem("u_mm"), sem("u_done")
        style_done, demod_mm, demod_read, wmod_done = sem("style_done"), sem("demod_mm"), sem("demod_read"), sem("wmod_done")
        t_mm, t_hi, t_done = sem("t_mm"), sem("t_hi"), sem("t_done")
        proj_mm, k_hi, k_done, v_done, hs_done = sem("proj_mm"), sem("k_hi"), sem("k_done"), sem("v_done"), sem("hs_done")
        q_mm, q_hi, s1_mm, mx_done = sem("q_mm"), sem("q_hi"), sem("s1_mm"), sem("mx_done")
        negm_mm, q_done, s2_mm, exp_done = sem("negm_mm"), sem("q_done"), sem("s2_mm"), sem("exp_done")
        av_mm, ao_done = sem("av_mm"), sem("ao_done")
        mo_mm, mo_done, mo_split = sem("mo_mm"), sem("mo_done"), sem("mo_split")
        rt_mm, rt_sub, rt_exp, parts_done = sem("rt_mm"), sem("rt_sub"), sem("rt_exp"), sem("parts_done")
        parts_tr, comb_done, b2_mm, acc_init = sem("parts_tr"), sem("comb_done"), sem("b2_mm"), sem("acc_init")
        w_done, h_mm, gelu_done, hi_done, lo_done, y_mm = (
            sem("w_done"), sem("h_mm"), sem("gelu_done"), sem("hi_done"), sem("lo_done"), sem("y_mm"))
        cb_mm, cb_read, weighted_done, acc_done, x1_done = (
            sem("cb_mm"), sem("cb_read"), sem("weighted_done"), sem("acc_done"), sem("x1_done"))
        kx_mm, kx_done, sub_done, soft_exp, a_done, prod_near, prod_far = (
            sem("kx_mm"), sem("kx_done"), sem("sub_done"), sem("soft_exp"), sem("a_done"), sem("prod_near"), sem("prod_far"))
        att_mm, att_read = sem("att_mm"), sem("att_read")
        out_done, mo_tile, acc_zero = sem("out_done"), sem("mo_tile"), sem("acc_zero")
        dve_chain, pool_chain = sem("dve_chain"), sem("pool_chain")

        block = ctx.enter_context(nc.Block())

        UNITS = [(kind, half, i) for half in range(HALVES)
                 for kind, n in (("k", GROUPS), ("v", PER_HALF), ("hs", 1)) for i in range(n)]
        PROJ_BANKS = [3, 4, 5, 6, 7]

        def unit_free(u):
            kind = UNITS[u][0]
            n = sum(1 for x in UNITS[:u + 1] if x[0] == kind)
            return {"k": k_done, "v": v_done, "hs": hs_done}[kind], n

        @block.sync
        def _(sp):
            sp.dma_start(projp, proj_pack[:]).then_inc(ld_proj, 16)
            sp.dma_start(condp, cond_pack[:]).then_inc(ld_cond, 16)
            sp.dma_start(projb, proj_bias[:]).then_inc(ld_proj, 16)
            sp.dma_start(xT[:], x_t[:]).then_inc(ld_cond, 16)
            sp.dma_start(const[:], const_pack[:]).then_inc(ld_const, 16)
            sp.dma_start(selp[:], sel_pack[:]).then_inc(ld_const, 16)
            for k in range(2 * E):
                if k >= 2:
                    sp.wait_ge(w_done, k - 1)
                layer, e = divmod(k, E)
                w = (w_layer0, w_layer1)[layer]
                width = 2 * CHUNKS[layer] * 128
                sp.dma_start(raw[:, k % 2, 0:width], w[:, e, :]).then_inc(ld_w[k % 2], 16)
            for half in range(HALVES):
                sp.wait_ge(out_done, half + 1)
                sp.dma_start(out[:, half * HALF:(half + 1) * HALF],
                             xhs[:, half * HALF:(half + 1) * HALF]).then_inc(stored, 16)
            sp.wait_ge(stored, 16 * HALVES)

        @block.tensor
        def _(pe):
            def mm(dst, lhs, rhs, start=True, stop=True, **kw):
                return nc.tensor.matmul(dst, lhs, rhs, start=start, stop=stop, **kw)

            pe.wait_ge(ld_proj, 32)
            for j in range(3):
                mm(bank[1 + j][:], projp[:, 0:128], projp[:, 128 + 512 * j:640 + 512 * j]).then_inc(wstack_mm, 1)
            pe.wait_ge(ld_cond, 32)
            cond = CP("cond")
            a = COND_AT["wdec"][0]
            for k in range(RANK):
                mm(bank[0][:, 8 * k:8 * k + 8], condp[:, a + D * k:a + D * (k + 1)], cond)
            mm(bank[0][:, 240:248], CP("ubias"), cond)
            mm(bank[0][:, 248:256], CP("kaff"), cond)
            mm(bank[0][:, 256:264], CP("oaff"), cond).then_inc(u_mm, 1)
            pe.wait_ge(u_done, 1)
            pe.wait_ge(wstack_done, 3)
            for b in range(BATCH):
                m = mm(bank[1 + b // PER_HALF][:, SEQ * (b % PER_HALF):SEQ * (b % PER_HALF + 1)],
                       urep[:, b, :, :].rearrange("p a b -> p (a b)"), xT[:, SEQ * b:SEQ * (b + 1)])
                if b % PER_HALF == PER_HALF - 1:
                    m.then_inc(t_mm, 1)
            pe.wait_ge(style_done, 1)
            for w in range(2):
                for b in range(BATCH):
                    m = mm(bank[4 + 2 * w + b // PER_HALF][:, SEQ * (b % PER_HALF):SEQ * (b % PER_HALF + 1)],
                           style2[:, w, b:b + 1].to_broadcast([128, 128]), wsq[:, w, :])
                    if b % PER_HALF == PER_HALF - 1:
                        m.then_inc(demod_mm, 1)
            for u, (kind, half, i) in enumerate(UNITS):
                if u == 0 or UNITS[u - 1][1] != half:
                    pe.wait_ge(t_done, half + 1)
                if u == 1:
                    pe.wait_ge(demod_read, 4)
                if u >= len(PROJ_BANKS):
                    pe.wait_ge(*unit_free(u - len(PROJ_BANKS)))
                dst = bank[PROJ_BANKS[u % len(PROJ_BANKS)]]
                tokens = slice(half * HALF, (half + 1) * HALF)
                if kind == "k":
                    m = mm(dst[:], wst[:, 1, 128 * i:128 * (i + 1)], ts[:, tokens])
                elif kind == "v":
                    b = half * PER_HALF + i
                    m = mm(dst[:], ts[:, SEQ * b:SEQ * (b + 1)], wst[:, 2, :])
                else:
                    m = mm(dst[:], vst[:], ts[:, tokens])
                m.then_inc(proj_mm, 1)

            def queries(b):
                if b >= 2:
                    pe.wait_ge(q_done, b - 1)
                for G in range(GROUPS):
                    m = mm(bank[1 + b % 2][:, 128 * G:128 * (G + 1)], wst[:, 0, 128 * G:128 * (G + 1)],
                           ts[:, SEQ * b:SEQ * (b + 1)], start=G == 0, stop=False, skip_group_check=True)
                m.then_inc(q_mm, 1)

            def first_scores(b, r):
                if b >= 1:
                    pe.wait_ge(exp_done, 4 * (b - 1) + r + 1)
                rows = slice(32 * r, 32 * r + 8)
                for G in range(GROUPS):
                    m = mm(bank[3 + r][:, 128 * G:128 * (G + 1)], hi16[rows, b % 2, 128 * G:128 * (G + 1)],
                           kop[rows, G, SEQ * b:SEQ * (b + 1)], tile_position=(32 * r, 0))
                m.then_inc(s1_mm, 1)

            queries(0)
            for u in range(len(UNITS) - len(PROJ_BANKS), len(UNITS)):
                pe.wait_ge(*unit_free(u))
            pe.wait_ge(q_hi, 1)
            for r in range(4):
                first_scores(0, r)
            for b in range(BATCH):
                if b + 1 < BATCH:
                    queries(b + 1)
                pe.wait_ge(mx_done, 4 * (b + 1))
                for G in range(GROUPS):
                    m = mm(bank[1 + b % 2][:, 128 * G:128 * (G + 1)], negm[:, b % 2, G, :], ident16[:],
                           start=False, stop=G == GROUPS - 1, skip_group_check=True)
                m.then_inc(negm_mm, 1)
                pe.wait_ge(q_done, b + 1)
                for r in range(4):
                    rows = slice(32 * r, 32 * r + 32)
                    for G in range(GROUPS):
                        m = mm(bank[3 + r][:, 128 * G:128 * (G + 1)], kop[rows, G, SEQ * b:SEQ * (b + 1)],
                               qop[rows, b % 2, 128 * G:128 * (G + 1)], tile_position=(32 * r, 0))
                    m.then_inc(s2_mm, 1)
                if b + 1 < BATCH:
                    pe.wait_ge(q_hi, b + 2)
                if b >= 1:
                    pe.wait_ge(ao_done, b)
                for r in range(4):
                    if b + 1 < BATCH:
                        first_scores(b + 1, r)
                    else:
                        pe.wait_ge(exp_done, 4 * b + r + 1)
                    for G in range(GROUPS):
                        cols = slice(128 * G, 128 * (G + 1))
                        h = 4 * G + r
                        mm(bank[7][32 * r:32 * r + 32, cols], val[:, b, 32 * h:32 * h + 32],
                           probs[:, b % 2, r, cols], tile_position=(0, 32 * r))
                        m = mm(bank[0][32 * r:32 * r + 32, cols], ones32[:],
                               probs[:, b % 2, r, cols], tile_position=(0, 32 * r))
                m.then_inc(av_mm, 1)
            for half in range(HALVES):
                pe.wait_ge(ao_done, PER_HALF * (half + 1))
                for G in range(GROUPS):
                    a = CONST_AT["ow"][0] + D * G
                    m = mm(bank[5 + half][:], const[:, a:a + D], ao[:, G, half * HALF:(half + 1) * HALF],
                           start=G == 0, stop=G == GROUPS - 1)
                m.then_inc(mo_mm, 1)

            def route(layer):
                for half in range(HALVES):
                    n = layer * HALVES + half
                    pe.wait_ge(mo_done, n + 1)
                    if layer == 0 and half == 0:
                        pe.wait_ge(ao_done, BATCH)
                    if half == 1 or layer == 1:
                        pe.wait_ge(comb_done if layer == 1 else acc_init, n if layer == 1 else half)
                    for t in range(PER_HALF):
                        m = mm(bank[0][:, E * t:E * (t + 1)],
                               mo[:, half * HALF + SEQ * t:half * HALF + SEQ * (t + 1)], C(f"rw{layer}"))
                    m.then_inc(rt_mm, 1)
                    pe.wait_ge(parts_done, n + 1)
                    for t in range(PER_HALF):
                        m = nc.tensor.transpose(bank[0][0:16, 128 * t:128 * (t + 1)],
                                                parts[:, t, :].bitcast(F32), C("ident"))
                    m.then_inc(parts_tr, 1)
                    if layer == 0:
                        pe.wait_ge(comb_done, n + 1)
                        mm(bank[0][:], selp[:, E * 128:], comb_t[:, half, :].bitcast(F32)).then_inc(b2_mm, 1)

            def first_product(c):
                j, fc = CHUNK_LIST[c]
                layer, e, half = JOBS[j]
                k = layer * E + e
                if fc == 0:
                    if j >= 2:
                        pe.wait_ge(cb_read, j - 1)
                    mm(bank[5 + j % 2][:], sel[:, 128 * e:128 * (e + 1)], comb_t[:, half, :]).then_inc(cb_mm, 1)
                    pe.wait_ge(w_done, k + 1)
                if c >= 3:
                    pe.wait_ge(gelu_done, c - 2)
                tokens = slice(half * HALF, (half + 1) * HALF)
                at = slice(128 * fc, 128 * (fc + 1))
                dst = bank[1 + c % 3][:]
                mm(dst, w_hi[:, k % 3, at], mo_hi[:, tokens], stop=False)
                mm(dst, w_hi[:, k % 3, at], mo_lo[:, tokens], start=False, stop=False)
                mm(dst, w_lo[:, k % 3, at], mo_hi[:, tokens], start=False).then_inc(h_mm, 1)

            def second_product(c):
                j, fc = CHUNK_LIST[c]
                layer, e, half = JOBS[j]
                k = layer * E + e
                n = CHUNKS[layer]
                if fc == 0 and j >= 2:
                    pe.wait_ge(weighted_done, j - 1)
                pe.wait_ge(lo_done, c + 1)
                at = slice(128 * (n + fc), 128 * (n + fc + 1))
                dst = bank[(4, 7)[j % 2]][:]
                mm(dst, w_hi[:, k % 3, at], g_hi[:, c % 3, :], start=fc == 0, stop=False)
                mm(dst, w_hi[:, k % 3, at], g_lo[:, c % 3, :], start=False, stop=False)
                mm(dst, w_lo[:, k % 3, at], g_hi[:, c % 3, :], start=False, stop=fc == n - 1).then_inc(y_mm, 1)

            def experts(layer):
                first, end = FIRST_CHUNK[layer * JOBS_PER_LAYER], END_CHUNK[(layer + 1) * JOBS_PER_LAYER - 1]
                pe.wait_ge(mo_split, HALVES * (layer + 1))
                pe.wait_ge(comb_done, HALVES * (layer + 1))
                for c in range(first, end + LAG):
                    if c < end:
                        first_product(c)
                    if c - LAG >= first:
                        second_product(c - LAG)

            route(0)
            experts(0)

            def keys(b):
                if b % PER_HALF == 0:
                    pe.wait_ge(x1_done, b // PER_HALF + 1)
                if b == 0:
                    pe.wait_ge(wmod_done, 1)
                if b >= 2:
                    pe.wait_ge(kx_done, b - 1)
                mm(bank[1 + b % 2][:, 0:128], x1[:, SEQ * b:SEQ * (b + 1)], wmod[:, 0, b, :]).then_inc(kx_mm, 1)

            def output(b):
                pe.wait_ge(att_read, b + 1)
                m = mm(bank[5 + b // PER_HALF][:, SEQ * (b % PER_HALF):SEQ * (b % PER_HALF + 1)],
                       wmod[:, 1, b, :], att_t[:, b % 2, :])
                m.then_inc(mo_tile, 1)

            keys(0)
            for b in range(BATCH):
                if b + 1 < BATCH:
                    keys(b + 1)
                if b >= 1:
                    output(b - 1)
                pe.wait_ge(prod_near, b + 1)
                pe.wait_ge(prod_far, b + 1)
                if b >= 2:
                    pe.wait_ge(att_read, b - 1)
                for s in range(H1):
                    m = mm(bank[3 + b % 2][:, 0:128], prod[:, b % 2, 128 * s:128 * (s + 1)], C("ident"),
                           start=s == 0, stop=s == H1 - 1)
                m.then_inc(att_mm, 1)
            output(BATCH - 1)
            route(1)
            experts(1)

        @block.scalar
        def _(act):
            def activate(dst, src, func, **kw):
                return nc.scalar.activation(dst, src, func, **kw)

            act.wait_ge(consts_made, 1)
            for n in range(4):
                act.wait_ge(demod_mm, n + 1)
                activate(demod[:, n // 2, (n % 2) * HALF:(n % 2 + 1) * HALF], bank[4 + n][:], ACT.Sqrt,
                         bias=eps[:]).then_inc(demod_read, 1)
            for b in range(BATCH):
                if b % PER_HALF == 0:
                    act.wait_ge(t_mm, b // PER_HALF + 1)
                activate(ts[:, SEQ * b:SEQ * (b + 1)],
                         bank[1 + b // PER_HALF][:, SEQ * (b % PER_HALF):SEQ * (b % PER_HALF + 1)],
                         ACT.Identity, bias=ubias[:, b:b + 1]).then_inc(t_hi, 1)
            nk = 0
            for u, (kind, half, i) in enumerate(UNITS):
                src = bank[PROJ_BANKS[u % len(PROJ_BANKS)]][:]
                if kind == "hs":
                    continue
                act.wait_ge(proj_mm, u + 1)
                if kind == "k":
                    if nk >= 2:
                        act.wait_ge(k_done, nk - 1)
                    activate(hi16[:, nk % 2, :], src, ACT.Copy).then_inc(k_hi, 1)
                    nk += 1
                else:
                    activate(val[:, half * PER_HALF + i, :], src, ACT.Copy).then_inc(v_done, 1)

            def query_parts(b):
                act.wait_ge(q_mm, b + 1)
                if b < 2:
                    act.wait_ge(k_done, GROUPS * HALVES)
                else:
                    act.wait_ge(q_done, b - 1)
                activate(hi16[:, b % 2, :], bank[1 + b % 2][:], ACT.Copy).then_inc(q_hi, 1)

            query_parts(0)
            act.wait_ge(wmod_done, 1)
            for b in range(BATCH):
                if b + 1 < BATCH:
                    query_parts(b + 1)
                for r in range(4):
                    act.wait_ge(s2_mm, 4 * b + r + 1)
                    if b >= 2 and r == 0:
                        act.wait_ge(av_mm, b - 1)
                    activate(probs[:, b % 2, r, :], bank[3 + r][:], ACT.Exp,
                             scale=float(KPH) ** -0.5).then_inc(exp_done, 1)

            def block_output(layer, half):
                n = layer * HALVES + half
                if layer == 0:
                    act.wait_ge(mo_mm, half + 1)
                else:
                    act.wait_ge(mo_tile, PER_HALF * (half + 1))
                activate(mo[:, half * HALF:(half + 1) * HALF], bank[5 + half][:], ACT.Identity,
                         bias=C(f"ob{layer}")).then_inc(mo_done, 1)

            def routing(layer):
                for half in range(HALVES):
                    n = layer * HALVES + half
                    act.wait_ge(rt_sub, n + 1)
                    activate(rt[:, 1, :, :], rt[:, 0, :, :], ACT.Exp).then_inc(rt_exp, 1)

            def experts(layer):
                for c in range(FIRST_CHUNK[layer * JOBS_PER_LAYER], END_CHUNK[(layer + 1) * JOBS_PER_LAYER - 1]):
                    j, fc = CHUNK_LIST[c]
                    _, e, half = JOBS[j]
                    act.wait_ge(h_mm, c + 1)
                    if c >= 3:
                        act.wait_ge(lo_done, c - 2)
                    if layer == 0:
                        a = CONST_AT["b1"][0] + CHUNKS[0] * e + fc
                        activate(g[:, c % 3, :], bank[1 + c % 3][:], ACT.Gelu, bias=const[:, a:a + 1]).then_inc(gelu_done, 1)
                    else:
                        activate(g[:, c % 3, :], bank[1 + c % 3][:], ACT.Gelu).then_inc(gelu_done, 1)
                    if fc == 0:
                        act.wait_ge(cb_mm, j + 1)
                        if j >= 2:
                            act.wait_ge(weighted_done, j - 1)
                        activate(cbs[:, j % 2, :], bank[5 + j % 2][:], ACT.Copy).then_inc(cb_read, 1)

            for half in range(HALVES):
                block_output(0, half)
            routing(0)
            experts(0)

            def soft(b):
                act.wait_ge(sub_done, b + 1)
                activate(amat[:, b % 2, :, :], amat[:, b % 2, :, :], ACT.Exp,
                         scale=float(D1) ** -0.5).then_inc(soft_exp, 1)

            soft(0)
            for b in range(BATCH):
                if b + 1 < BATCH:
                    soft(b + 1)
                act.wait_ge(att_mm, b + 1)
                if b >= 2:
                    act.wait_ge(mo_tile, b - 1)
                activate(att_t[:, b % 2, :], bank[3 + b % 2][:, 0:128], ACT.Copy).then_inc(att_read, 1)
                if b % PER_HALF == PER_HALF - 1 and b + 1 < BATCH:
                    pass
            for half in range(HALVES):
                block_output(1, half)
            routing(1)
            experts(1)

        @block.vector
        def _(dve):
            v = nc.vector
            linked = [0]

            def link(ins):
                ins.then_inc(dve_chain, 1)
                linked[0] += 1
                dve.wait_ge(dve_chain, linked[0])

            link(v.memset(urep[:], 0.0))
            v.memset(negm[:], 0.0)
            v.memset(ones32[:], 1.0)
            link(v.memset(eps[:], DEMOD_EPS))
            dve.wait_ge(ld_proj, 32)
            for j in range(3):
                dve.wait_ge(wstack_mm, j + 1)
                link(v.tensor_tensor(wfull[:], bank[1 + j][:], projb[:, 512 * j:512 * (j + 1)], ALU.add))
                link(v.tensor_copy(wst[:, j, :], wfull[:]))
                for rows in (slice(32, 64), slice(96, 128)):
                    ins = v.tensor_tensor(wst[rows, j, :], wfull[rows, :], wst[rows, j, :].bitcast(F32), ALU.subtract)
                    if rows.start == 96:
                        ins.then_inc(wstack_done, 1)
                        dve.wait_ge(wstack_done, j + 1)
            dve.wait_ge(ld_const, 32)
            link(v.tensor_copy(vst[:], C("vrep")))
            for rows in (slice(32, 64), slice(96, 128)):
                v.tensor_tensor(vst[rows, :], C("vrep")[rows, :], vst[rows, :].bitcast(F32), ALU.subtract)
            v.tensor_copy(ident16[:], C("ident"))
            link(v.tensor_copy(sel[:], selp[:, 0:E * 128]))
            for w, name in enumerate(("wk", "wo")):
                v.tensor_tensor(wsq[:, w, :], C(name), C(name), ALU.mult)
            dve.wait_ge(u_mm, 1)
            for blk in range(4):
                v.tensor_copy(urep[:, :, blk, 0:RANK], view(bank[0], 0, [[1, BATCH], [8, RANK]]))
            v.tensor_copy(ubias[:], bank[0][:, 240:248])
            link(v.tensor_copy(style[:].rearrange("p w b -> p (w b)"), bank[0][:, 248:264]))
            v.tensor_tensor(style2[:], style[:], style[:], ALU.mult).then_inc(u_done, 1)
            dve.wait_ge(u_done, 1)
            v.tensor_copy(rs[:, 0, 0, :], style2[:, 0, 0:1]).then_inc(style_done, 1)
            for b in range(BATCH):
                dve.wait_ge(t_hi, PER_HALF * (b // PER_HALF + 1))
                cols = slice(SEQ * b, SEQ * (b + 1))
                ins = v.scalar_tensor_tensor(
                    ts[64:128, cols], bank[1 + b // PER_HALF][64:128, SEQ * (b % PER_HALF):SEQ * (b % PER_HALF + 1)],
                    ubias[64:128, b:b + 1], ts[64:128, cols].bitcast(F32), ALU.add, ALU.subtract)
                if b % PER_HALF == PER_HALF - 1:
                    ins.then_inc(t_done, 1)
            nk = 0
            for u, (kind, half, i) in enumerate(UNITS):
                src = bank[PROJ_BANKS[u % len(PROJ_BANKS)]][:]
                tokens = slice(half * HALF, (half + 1) * HALF)
                if kind == "k":
                    nk += 1
                    dve.wait_ge(k_hi, nk)
                    v.scalar_tensor_tensor(kop[:, i, tokens], hi16[:, (nk - 1) % 2, :], C("mk"), src,
                                           ALU.mult, ALU.add).then_inc(k_done, 1)
                elif kind == "hs":
                    dve.wait_ge(proj_mm, u + 1)
                    v.tensor_tensor(xhs[:, tokens], src, xT[:, tokens], ALU.add).then_inc(hs_done, 1)
            dve.wait_ge(demod_read, 4)
            link(v.reciprocal(demod[:, :, :], demod[:, :, :]))
            for w, name in enumerate(("wk", "wo")):
                for b in range(BATCH):
                    ins = v.scalar_tensor_tensor(wmod[:, w, b, :], C(name), style[:, w, b:b + 1],
                                                 demod[:, w, SEQ * b:SEQ * (b + 1)], ALU.mult, ALU.mult)
            ins.then_inc(wmod_done, 1)

            def normalise(b):
                dve.wait_ge(av_mm, b + 1)
                link(v.reciprocal(rz[:], bank[0][:]))
                v.tensor_tensor(ao[:, :, SEQ * b:SEQ * (b + 1)], bank[7][:].rearrange("p (g s) -> p g s", g=GROUPS),
                                rz[:].rearrange("p (g s) -> p g s", g=GROUPS), ALU.mult).then_inc(ao_done, 1)
                dve.wait_ge(ao_done, b + 1)

            for b in range(BATCH):
                for r in range(4):
                    dve.wait_ge(s1_mm, 4 * b + r + 1)
                    if b >= 2 and r == 0:
                        dve.wait_ge(negm_mm, b - 1)
                    v.tensor_reduce(negm[:, b % 2, :, 32 * r + 16:32 * r + 17],
                                    bank[3 + r][:].rearrange("p (g t) -> p g t", g=GROUPS),
                                    AX.X, ALU.max, negate=True).then_inc(mx_done, 1)
                dve.wait_ge(negm_mm, b + 1)
                dve.wait_ge(q_hi, b + 1)
                v.scalar_tensor_tensor(qop[:, b % 2, :], hi16[:, b % 2, :], C("mq"), bank[1 + b % 2][:],
                                       ALU.mult, ALU.add).then_inc(q_done, 1)
                if b >= 1:
                    normalise(b - 1)
            normalise(BATCH - 1)

            def split_output(layer):
                for half in range(HALVES):
                    n = layer * HALVES + half
                    tokens = slice(half * HALF, (half + 1) * HALF)
                    dve.wait_ge(mo_done, n + 1)
                    link(v.tensor_copy(mo_hi[:, tokens], mo[:, tokens]))
                    v.tensor_tensor(mo_lo[:, tokens], mo[:, tokens], mo_hi[:, tokens].bitcast(F32),
                                    ALU.subtract).then_inc(mo_split, 1)

            def routing(layer):
                for half in range(HALVES):
                    n = layer * HALVES + half
                    wide = [128, PER_HALF, E]
                    logits, p, one, key, two, rest = (rt[:, i, :, :] for i in (0, 1, 2, 3, 4, 5))
                    top, inv, most, second = (rs[:, i, :, :] for i in (0, 1, 2, 3))
                    src = bank[0][:, 0:PER_HALF * E].rearrange("p (t e) -> p t e", t=PER_HALF)
                    dve.wait_ge(rt_mm, n + 1)
                    if layer == 0:
                        link(v.tensor_tensor(logits, src, C("rb").rearrange("p (t e) -> p t e", t=PER_HALF), ALU.add))
                    else:
                        link(v.tensor_copy(logits, src))
                    link(v.tensor_reduce(top, logits, AX.X, ALU.max))
                    v.tensor_tensor(logits, logits, top.to_broadcast(wide), ALU.subtract).then_inc(rt_sub, 1)
                    dve.wait_ge(rt_exp, n + 1)
                    link(v.tensor_reduce(inv, p, AX.X, ALU.add))
                    link(v.reciprocal(inv, inv))
                    link(v.tensor_tensor(p, p, inv.to_broadcast(wide), ALU.mult))
                    rank = C("rank").rearrange("p (t e) -> p t e", t=PER_HALF)

                    def pick(dst, values, largest):
                        link(v.tensor_reduce(largest, values, AX.X, ALU.max))
                        link(v.tensor_tensor(key, values, largest.to_broadcast(wide), ALU.is_equal))
                        link(v.tensor_tensor(key, key, rank, ALU.mult))
                        link(v.tensor_reduce(most, key, AX.X, ALU.max))
                        link(v.tensor_tensor(dst, key, most.to_broadcast(wide), ALU.is_equal))

                    pick(one, p, top)
                    link(v.scalar_tensor_tensor(rest, one, -2.0, p, ALU.mult, ALU.add))
                    pick(two, rest, second)
                    link(v.tensor_tensor(one, one, top.to_broadcast(wide), ALU.mult))
                    link(v.tensor_tensor(two, two, second.to_broadcast(wide), ALU.mult))
                    link(v.tensor_tensor(inv, top, second, ALU.add))
                    if layer == 0:
                        link(v.tensor_scalar(inv, inv, TOP_EPS, None, ALU.add))
                    link(v.reciprocal(inv, inv))
                    link(v.tensor_tensor(one, one, two, ALU.add))
                    link(v.tensor_tensor(one, one, inv.to_broadcast(wide), ALU.mult))
                    link(v.tensor_copy(parts[:, :, 0:E], one))
                    v.tensor_tensor(parts[:, :, E:2 * E], one, parts[:, :, 0:E].bitcast(F32),
                                    ALU.subtract).then_inc(parts_done, 1)
                    dve.wait_ge(parts_tr, n + 1)
                    v.tensor_copy(comb_t[:, half, :], bank[0][0:16, :]).then_inc(comb_done, 1)
                    if layer == 0:
                        dve.wait_ge(b2_mm, half + 1)
                        v.tensor_copy(acc[:, half * HALF:(half + 1) * HALF], bank[0][:]).then_inc(acc_init, 1)

            def weigh(j):
                dve.wait_ge(y_mm, END_CHUNK[j])
                dve.wait_ge(cb_read, j + 1)
                if j >= 2:
                    dve.wait_ge(acc_done, j - 1)
                v.tensor_tensor(weighted[:, j % 2, :], bank[(4, 7)[j % 2]][:], cbs[:, j % 2, :],
                                ALU.mult).then_inc(weighted_done, 1)

            def experts(layer):
                first, end = FIRST_CHUNK[layer * JOBS_PER_LAYER], END_CHUNK[(layer + 1) * JOBS_PER_LAYER - 1]
                for c in range(first, end + LAG):
                    if c < end:
                        dve.wait_ge(gelu_done, c + 1)
                        if c >= 3:
                            dve.wait_ge(y_mm, c - 2)
                        v.tensor_copy(g_hi[:, c % 3, :], g[:, c % 3, :]).then_inc(hi_done, 1)
                        dve.wait_ge(hi_done, c + 1)
                        v.tensor_tensor(g_lo[:, c % 3, :], g[:, c % 3, :], g_hi[:, c % 3, :].bitcast(F32),
                                        ALU.subtract).then_inc(lo_done, 1)
                    d = c - LAG
                    if first <= d and END_CHUNK[CHUNK_LIST[d][0]] == d + 1:
                        weigh(CHUNK_LIST[d][0])

            split_output(0)
            routing(0)
            experts(0)
            for half in range(HALVES):
                tokens = slice(half * HALF, (half + 1) * HALF)
                dve.wait_ge(acc_done, JOBS_PER_LAYER)
                v.scalar_tensor_tensor(x1[:, tokens], acc[:, tokens], MOE_SCALE, xhs[:, tokens],
                                       ALU.mult, ALU.add).then_inc(x1_done, 1)

            def scores(b):
                i = b % 2
                dve.wait_ge(kx_mm, b + 1)
                if b >= 2:
                    dve.wait_ge(prod_far, b - 1)
                v.tensor_tensor(kx2[:, i, 0:128], bank[1 + i][:, 0:128], C("kb"), ALU.add).then_inc(kx_done, 1)
                dve.wait_ge(kx_done, b + 1)
                link(v.tensor_copy(kx2[:, i, 128:256], kx2[:, i, 0:128]))
                link(v.tensor_tensor(dots.rearrange("p (s c) -> p s c", s=NEAR), view(kx2[:, i, :], 0, [[0, NEAR], [1, 128]]),
                                     view(kx2[:, i, :], 0, [[D1, NEAR], [1, 128]]), ALU.mult))
                link(v.tensor_reduce(gram[:, i, 0:NEAR, 0:H1], dots.rearrange("p (s h d) -> p s h d", s=NEAR, h=H1),
                                     AX.X, ALU.add))
                link(v.tensor_copy(gram[:, i, 1:H1 // 2, H1:2 * H1], gram[:, i, 1:H1 // 2, 0:H1]))
                link(v.tensor_copy(gram[:, i, NEAR:H1, 0:H1],
                                   view(gram[:, i, :, :], 2 * H1 + H1 - 1, [[2 * H1 - 1, H1 // 2 - 1], [1, H1]])))
                link(v.tensor_reduce(small[:, i, 0, :], gram[:, i, :, 0:H1].rearrange("p s h -> p h s"), AX.X, ALU.max))
                v.tensor_tensor(amat[:, i, :, :], gram[:, i, :, 0:H1], view(small[:, i, 0, :], 0, [[0, H1], [1, H1]]),
                                ALU.subtract).then_inc(sub_done, 1)

            def weights(b):
                i = b % 2
                dve.wait_ge(soft_exp, b + 1)
                link(v.tensor_reduce(small[:, i, 1, :], amat[:, i, :, :].rearrange("p s h -> p h s"), AX.X, ALU.add))
                link(v.reciprocal(small[:, i, 1, :], small[:, i, 1, :]))
                v.tensor_tensor(amat[:, i, :, :], amat[:, i, :, :], view(small[:, i, 1, :], 0, [[0, H1], [1, H1]]),
                                ALU.mult).then_inc(a_done, 1)
                dve.wait_ge(a_done, b + 1)
                if b >= 2:
                    dve.wait_ge(att_mm, b - 1)
                v.tensor_tensor(prod[:, i, 0:NEAR * 128].rearrange("p (s h d) -> p s h d", s=NEAR, h=H1),
                                view(amat[:, i, :, :], 0, [[H1, NEAR], [1, H1], [0, D1]]),
                                view(kx2[:, i, :], 0, [[D1, NEAR], [D1, H1], [1, D1]]), ALU.mult).then_inc(prod_near, 1)

            scores(0)
            for b in range(BATCH):
                if b + 1 < BATCH:
                    scores(b + 1)
                weights(b)
            split_output(1)
            routing(1)
            experts(1)
            for half in range(HALVES):
                tokens = slice(half * HALF, (half + 1) * HALF)
                dve.wait_ge(acc_done, 2 * JOBS_PER_LAYER)
                v.tensor_tensor(xhs[:, tokens], acc[:, tokens], x1[:, tokens], ALU.add).then_inc(out_done, 1)

        @block.gpsimd
        def _(pool):
            p = nc.gpsimd

            p.memset(rz[:, 0:1], 0.0).then_inc(consts_made, 1)

            def split_weights(k):
                if k >= 2 * E:
                    return
                width = 2 * CHUNKS[k // E] * 128
                pool.wait_ge(ld_w[k % 2], 16 * (k // 2 + 1))
                if k >= 3:
                    pool.wait_ge(y_mm, END_CHUNK[(k - 3) * HALVES + HALVES - 1])
                p.tensor_copy(w_hi[:, k % 3, 0:width], raw[:, k % 2, 0:width]).then_inc(pool_chain, 1)
                pool.wait_ge(pool_chain, k + 1)
                p.tensor_tensor(w_lo[:, k % 3, 0:width], raw[:, k % 2, 0:width], w_hi[:, k % 3, 0:width].bitcast(F32),
                                ALU.subtract).then_inc(w_done, 1)

            def accumulate(j):
                half = JOBS[j][2]
                tokens = slice(half * HALF, (half + 1) * HALF)
                pool.wait_ge(weighted_done, j + 1)
                if j >= 1:
                    pool.wait_ge(acc_done, j)
                p.tensor_tensor(acc[:, tokens], acc[:, tokens], weighted[:, j % 2, :], ALU.add).then_inc(acc_done, 1)

            def layer_of_experts(layer):
                for e in range(E):
                    k = layer * E + e
                    split_weights(k + 2)
                    for half in range(HALVES):
                        accumulate(k * HALVES + half)

            split_weights(0)
            split_weights(1)
            pool.wait_ge(acc_init, HALVES)
            layer_of_experts(0)
            pool.wait_ge(x1_done, HALVES)
            p.memset(acc[:], 0.0).then_inc(acc_zero, 1)
            for b in range(BATCH):
                i = b % 2
                pool.wait_ge(a_done, b + 1)
                if b >= 2:
                    pool.wait_ge(att_mm, b - 1)
                p.tensor_tensor(prod[:, i, NEAR * 128:].rearrange("p (s h d) -> p s h d", s=H1 - NEAR, h=H1),
                                view(amat[:, i, :, :], H1 * NEAR, [[H1, H1 - NEAR], [1, H1], [0, D1]]),
                                view(kx2[:, i, :], D1 * (H1 - 1), [[-D1, H1 - NEAR], [D1, H1], [1, D1]]),
                                ALU.mult).then_inc(prod_far, 1)
            pool.wait_ge(acc_zero, 1)
            layer_of_experts(1)


def kernel(**inputs):
    import numpy as np
    import concourse.bacc as bacc
    from concourse.bass_utils import run_bass_kernel_spmd

    t = {k: np.asarray(v) for k, v in inputs.items()}
    f32 = np.float32

    cond = np.ones((COND + 1, BATCH), f32)
    cond[:COND] = t["cond_512"].T
    wdec = np.concatenate([t["L0_cond_W_dec"], t["L0_cond_b_dec"][None]], 0).reshape(COND + 1, D + 1, RANK)
    ubias = np.zeros((COND + 1, 4, 32), f32)
    ubias[:, :, :RANK] = wdec[:, D, None, :]
    ubias[COND, :, RANK] = 1.0
    kaff = np.concatenate([t["L1_cond_k_aff_w"].T, t["L1_cond_k_aff_b"][None]], 0)
    oaff = np.concatenate([t["L1_cond_o_aff_w"].T, t["L1_cond_o_aff_b"][None]], 0)
    cond_pack = np.concatenate([wdec[:, :D].transpose(0, 2, 1).reshape(COND + 1, RANK * D),
                                ubias.reshape(COND + 1, 128), cond, kaff, oaff], 1)

    V = t["L0_cond_V"]
    vrep = np.zeros((4, 32, D), f32)
    vrep[:, :RANK] = V[None]
    vrep = vrep.reshape(128, D)
    wq, wk, wv = (np.zeros((D, 512), f32) for _ in range(3))
    bias = np.zeros((4, 32, 3, 512), f32)
    for G in range(GROUPS):
        for r in range(4):
            h = 4 * G + r
            for part in range(4):
                at = 128 * G + 32 * r + 4 * part
                wq[:, at:at + 4] = t["L0_ffn_q_w"][:, 8 * h:8 * h + 4]
                wk[:, at:at + 4] = t["L0_ffn_k_w"][:, 4 * h:4 * h + 4]
                bias[:, RANK, 0, at:at + 4] = t["L0_ffn_q_b"][8 * h:8 * h + 4]
                bias[:, RANK, 1, at:at + 4] = t["L0_ffn_k_b"][4 * h:4 * h + 4]
            bias[:, RANK, 1, 128 * G + 32 * r + 16] = 1.0
            wv[:, 32 * h:32 * h + 4] = t["L0_ffn_v_w"][:, 4 * h:4 * h + 4]
            bias[:, RANK, 2, 32 * h:32 * h + 4] = t["L0_ffn_v_b"][4 * h:4 * h + 4]
    proj_pack = np.concatenate([vrep.T, wq, wk, wv], 1)
    proj_bias = bias.reshape(128, 1536)

    ow = np.zeros((4, 32, GROUPS, D), f32)
    for G in range(GROUPS):
        for r in range(4):
            h = 4 * G + r
            ow[r, :4, G] = t["L0_ffn_o_w"][4 * h:4 * h + 4]
    row = np.arange(128) % 32
    mq = np.where((row >= 8) & (row < 16), -1.0, 0.0).astype(f32)[:, None]
    mk = np.where((row < 16) & (row % 8 >= 4), -1.0, 0.0).astype(f32)[:, None]
    rank = np.tile(np.arange(E, 0, -1).astype(f32), (128, PER_HALF))
    const_pack = np.concatenate([
        vrep, np.eye(128, dtype=f32), t["L1_cond_k_w"].T, t["L1_cond_o_w"].T,
        np.tile(t["L1_cond_k_b"], (128, 1)), ow.reshape(128, GROUPS * D),
        t["L0_ffn_router_w"], t["L1_ffn_router_w"].T, np.tile(t["L0_ffn_router_b"], (128, PER_HALF)), rank,
        t["L0_ffn_b1"].reshape(E * CHUNKS[0], 128).T, t["L0_ffn_o_b"][:, None], t["L1_cond_o_b"][:, None], mq, mk], 1)
    sel = np.zeros((2, E, E, 128), f32)
    for e in range(E):
        sel[:, e, e] = 1.0
    sel_pack = np.concatenate([sel.reshape(16, E * 128), np.tile(t["L0_ffn_b2"], (2, 1))], 1)

    def expert_weights(w1, w2, chunks):
        return np.concatenate([w1.transpose(1, 0, 2), w2.reshape(E, chunks, 128, D).transpose(2, 0, 1, 3)
                               .reshape(128, E, chunks * D)], 2)

    arrays = {
        "cond_pack": cond_pack, "proj_pack": proj_pack, "proj_bias": proj_bias, "x_t": t["x"].reshape(TOK, D).T,
        "const_pack": const_pack, "sel_pack": sel_pack,
        "w_layer0": expert_weights(t["L0_ffn_w1"], t["L0_ffn_w2"], CHUNKS[0]),
        "w_layer1": expert_weights(t["L1_ffn_w1"], t["L1_ffn_w2"], CHUNKS[1]),
    }
    nc = bacc.Bacc("TRN2", target_bir_lowering=False, num_devices=1)
    feed, args = {}, []
    for name, a in arrays.items():
        a = np.ascontiguousarray(a)
        feed[f"in_{name}"] = a
        args.append(nc.dram_tensor(f"in_{name}", a.shape, mybir.dt.from_np(a.dtype), kind="ExternalInput").ap())
    args.append(nc.dram_tensor("out_t", (D, TOK), F32, kind="ExternalOutput").ap())
    program(nc, *args)
    r = run_bass_kernel_spmd(nc, [feed], core_ids=[0])
    return np.ascontiguousarray(r.results[0]["out_t"].T).reshape(BATCH, SEQ, D)
```

```python
from contextlib import ExitStack

import concourse.bass as bass
from concourse import mybir

BATCH, SEQ, D = 8, 128, 128
TOK = BATCH * SEQ
HALF = 512
HALVES = TOK // HALF
PER_HALF = HALF // SEQ
COND = 64
RANK = 30
HEADS, KPH = 16, 4
GROUPS = HEADS // 4
E = 8
CHUNKS = (256 // 128, 512 // 128)
H1, D1 = 16, D // 16
NEAR = H1 // 2 + 1
MOE_SCALE = 0.3
DEMOD_EPS = 1e-8
TOP_EPS = 1e-8

F32 = mybir.dt.float32
FR = mybir.dt.float32r
F16 = mybir.dt.float16
ALU = mybir.AluOpType
ACT = mybir.ActivationFunctionType
AX = mybir.AxisListType


def columns(*fields):
    at, found = 0, {}
    for name, width in fields:
        found[name] = (at, at + width)
        at += width
    return found, at


COND_AT, COND_W = columns(("wdec", RANK * D), ("ubias", 128), ("cond", BATCH), ("kaff", D), ("oaff", D))
QKV = 3 * HEADS * KPH
PROJ_AT, PROJ_W = columns(("vt", 128), ("w", QKV), ("bias", QKV), ("one", 1), ("mq", 1), ("mk", 1), ("vrep", 128))
CONST_AT, CONST_W = columns(
    ("ident", 128), ("wk", D), ("wk_t", D), ("wo_t", D), ("kb", D), ("ow", GROUPS * D), ("rw0", E), ("rw1", E),
    ("rb", BATCH * E), ("rank", BATCH * E), ("b1", E * CHUNKS[0]), ("ob0", 1), ("ob1", 1))

JOBS = [(layer, e, half) for layer in range(2) for e in range(E) for half in range(HALVES)]
CHUNK_LIST = [(j, fc) for j, (layer, _, _) in enumerate(JOBS) for fc in range(CHUNKS[layer])]
FIRST_CHUNK = {j: c for c, (j, fc) in enumerate(CHUNK_LIST) if fc == 0}
END_CHUNK = {j: c + 1 for c, (j, fc) in enumerate(CHUNK_LIST)}
JOBS_PER_LAYER = E * HALVES
LAG = 2


def program(nc, cond_pack, proj_pack, x_t, const_pack, sel_pack, w_layer0, w_layer1, out):
    with ExitStack() as ctx:
        def sb(name, shape, dt=F32):
            return ctx.enter_context(nc.sbuf_tensor(name, shape, dt))

        def sem(name):
            return ctx.enter_context(nc.semaphore(name))

        bank = [ctx.enter_context(nc.psum_tensor(f"bank{i}", [128, 512], F32)) for i in range(8)]

        early = sb("early", [128, COND_W])
        condp = early[0:COND + 1, :]
        ao = early[:, 0:GROUPS * TOK].rearrange("p (g n) -> p g n", g=GROUPS)
        projp = sb("projp", [128, PROJ_W])
        g = sb("g", [128, 3, 512])
        cbs = sb("cbs", [128, 2, 512])
        xT = sb("xT", [128, TOK])
        const = sb("const", [128, CONST_W])
        selp = sb("selp", [16, E * 128 + 128])
        raw = sb("raw", [128, 2, 1024])

        def C(name):
            a, b = CONST_AT[name]
            return const[:, a:b]

        def PP(name):
            a, b = PROJ_AT[name]
            return projp[:, a:b]

        def CP(name):
            a, b = COND_AT[name]
            return condp[:, a:b]

        ones32 = sb("ones32", [128, 32])
        eps = sb("eps", [128, 1])
        ident16 = sb("ident16", [128, 128], F16)
        sel = sb("sel", [16, E * 128], FR)
        urep = sb("urep", [128, BATCH, 4, 32])
        ubias = sb("ubias", [128, 8])
        wfull = sb("wfull", [128, QKV])
        wc = sb("wc", [128, QKV], FR)
        wst = sb("wst", [128, 2, 512], FR)
        vst = sb("vst", [128, 128], FR)
        ts = sb("ts", [128, TOK], FR)
        hi16 = sb("hi16", [128, 2, 512], F16)
        kop = sb("kop", [128, GROUPS, TOK], F16)
        val = sb("val", [128, BATCH, 512])
        qop = sb("qop", [128, 2, 512], F16)
        negm = sb("negm", [128, 2, GROUPS, 128], F16)
        probs = sb("probs", [128, 2, 4, 512])
        rz = sb("rz", [128, 512])
        newton = sb("newton", [128, 512])
        xhs = sb("xhs", [128, TOK])
        mo = sb("mo", [128, TOK])
        mo_hi = sb("mo_hi", [128, TOK], FR)
        mo_lo = sb("mo_lo", [128, TOK], FR)
        w_hi = sb("w_hi", [128, 3 * 1024], FR)
        w_lo = sb("w_lo", [128, 3 * 1024], FR)
        g_hi = sb("g_hi", [128, 3, 512], FR)
        g_lo = sb("g_lo", [128, 3, 512], FR)
        weighted = sb("weighted", [128, 2, 512])
        acc = xT
        x1 = sb("x1", [128, TOK])
        rt = sb("rt", [128, 8, BATCH, E])
        rs = sb("rs", [128, 8, BATCH, 1])
        parts = sb("parts", [128, BATCH, 2 * E], FR)
        comb_t = sb("comb_t", [16, HALVES, HALF], FR)
        style = sb("style", [128, 2, BATCH])
        style2 = sb("style2", [128, 2, BATCH])
        wsq = sb("wsq", [128, 2, D])
        demod = sb("demod", [128, 2, BATCH])
        wmod = sb("wmod", [128, BATCH, D])
        kx2 = val[:, 0:4, :].rearrange("p a b -> p (a b)").rearrange("p (b c) -> p b c", b=BATCH)
        gram = val[:, 4:6, :].rearrange("p t (s h) -> p t s h", s=H1)
        amat = val[:, 6:8, :].rearrange("p i (t s h) -> p i t s h", t=2, s=H1)
        dots = early[:, 0:2 * NEAR * D]
        att_t = early[:, 2 * NEAR * D:2 * NEAR * D + 2 * SEQ].rearrange("p (i c) -> p i c", i=2)
        diag = probs[:, 0, 0:2, :].rearrange("p a b -> p (a b)").rearrange("p (b c) -> p b c", b=BATCH)
        prod = probs[:, :, :, :].rearrange("p i a b -> p i (a b)")
        small = sb("small", [128, 2, 2, 2, H1])

        def view(t, first, dims):
            a = t[:, ...] if not isinstance(t, bass.AP) else t
            return bass.AP(tensor=a.tensor, offset=a.offset + first, ap=[list(a.ap[0]), *[list(x) for x in dims]])

        ld_proj, ld_cond, ld_x, ld_const = sem("ld_proj"), sem("ld_cond"), sem("ld_x"), sem("ld_const")
        ld_w = [sem("ld_w_even"), sem("ld_w_odd")]
        stored = sem("stored")
        consts_made = sem("consts_made")
        wstack_mm, wstack_done = sem("wstack_mm"), sem("wstack_done")
        u_mm, u_done = sem("u_mm"), sem("u_done")
        demod_mm, demod_read, diag_done = sem("demod_mm"), sem("demod_read"), sem("diag_done")
        wmod_mm, wmod_done, wsq_done, val_clear = sem("wmod_mm"), sem("wmod_done"), sem("wsq_done"), sem("val_clear")
        t_mm, t_hi, t_done = sem("t_mm"), sem("t_hi"), sem("t_done")
        proj_mm, k_hi, k_done, v_done, hs_done = sem("proj_mm"), sem("k_hi"), sem("k_done"), sem("v_done"), sem("hs_done")
        q_mm, q_hi, s1_mm, mx_done = sem("q_mm"), sem("q_hi"), sem("s1_mm"), sem("mx_done")
        negm_mm, q_done, s2_mm, exp_done = sem("negm_mm"), sem("q_done"), sem("s2_mm"), sem("exp_done")
        av_mm, log_done, inv_done, ao_done = sem("av_mm"), sem("log_done"), sem("inv_done"), sem("ao_done")
        mo_mm, mo_done, mo_split = sem("mo_mm"), sem("mo_done"), sem("mo_split")
        rt_mm, rt_sub, rt_exp, parts_done = sem("rt_mm"), sem("rt_sub"), sem("rt_exp"), sem("parts_done")
        parts_tr, comb_done, b2_mm, acc_init = sem("parts_tr"), sem("comb_done"), sem("b2_mm"), sem("acc_init")
        w_done, h_mm, gelu_done, hi_done, lo_done, y_mm = (
            sem("w_done"), sem("h_mm"), sem("gelu_done"), sem("hi_done"), sem("lo_done"), sem("y_mm"))
        cb_mm, cb_read, weighted_done, acc_done, x1_done = (
            sem("cb_mm"), sem("cb_read"), sem("weighted_done"), sem("acc_done"), sem("x1_done"))
        kx_dup = sem("kx_dup")
        kx_mm, kx_done, sub_done, soft_exp, a_done, prod_near, prod_far = (
            sem("kx_mm"), sem("kx_done"), sem("sub_done"), sem("soft_exp"), sem("a_done"), sem("prod_near"), sem("prod_far"))
        att_mm, att_read = sem("att_mm"), sem("att_read")
        out_done, mo_tile, mo_tile_read, acc_zero = sem("out_done"), sem("mo_tile"), sem("mo_tile_read"), sem("acc_zero")
        dve_chain, pool_chain = sem("dve_chain"), sem("pool_chain")

        block = ctx.enter_context(nc.Block())

        def weight_slot(k):
            return 512 * (k % 6) if k < E else 1024 * ((k - E + 1) % 3)

        def slot_free(k):
            if k < E:
                return k - 6 if k >= 6 else None
            return {0: 3, 1: 5, 2: 7}.get(k - E, k - 3)

        UNITS = [(kind, half, i) for half in range(HALVES)
                 for kind, n in (("k", GROUPS), ("v", half), ("hs", 1)) for i in range(n)]
        PROJ_BANKS = [3, 4, 5, 6, 7]

        def unit_free(u):
            kind = UNITS[u][0]
            n = sum(1 for x in UNITS[:u + 1] if x[0] == kind)
            return {"k": k_done, "v": v_done, "hs": hs_done}[kind], n

        @block.sync
        def _(sp):
            sp.dma_start(condp, cond_pack[:]).then_inc(ld_cond, 16)
            sp.dma_start(projp[:], proj_pack[:]).then_inc(ld_proj, 16)
            sp.dma_start(xT[:], x_t[:]).then_inc(ld_x, 16)
            sp.dma_start(const[:], const_pack[:]).then_inc(ld_const, 16)
            sp.dma_start(selp[:], sel_pack[:]).then_inc(ld_const, 16)
            for k in range(2 * E):
                if k >= 2:
                    sp.wait_ge(w_done, k - 1)
                layer, e = divmod(k, E)
                w = (w_layer0, w_layer1)[layer]
                width = 2 * CHUNKS[layer] * 128
                sp.dma_start(raw[:, k % 2, 0:width], w[:, e, :]).then_inc(ld_w[k % 2], 16)
            for half in range(HALVES):
                sp.wait_ge(out_done, half + 1)
                sp.dma_start(out[:, half * HALF:(half + 1) * HALF],
                             xhs[:, half * HALF:(half + 1) * HALF]).then_inc(stored, 16)
            sp.wait_ge(stored, 16 * HALVES)

        @block.tensor
        def _(pe):
            def mm(dst, lhs, rhs, start=True, stop=True, **kw):
                return nc.tensor.matmul(dst, lhs, rhs, start=start, stop=stop, **kw)

            pe.wait_ge(ld_cond, 16)
            cond = CP("cond")
            a = COND_AT["wdec"][0]
            for k in range(RANK):
                mm(bank[0][:, 8 * k:8 * k + 8], condp[:, a + D * k:a + D * (k + 1)], cond)
            mm(bank[0][:, 240:248], CP("ubias"), cond)
            mm(bank[0][:, 248:256], CP("kaff"), cond)
            mm(bank[0][:, 256:264], CP("oaff"), cond).then_inc(u_mm, 1)
            pe.wait_ge(ld_proj, 16)
            mm(bank[3][:, 0:QKV], PP("vt"), PP("w")).then_inc(wstack_mm, 1)
            pe.wait_ge(u_done, 1)
            pe.wait_ge(ld_x, 16)
            for b in range(BATCH):
                m = mm(bank[1 + b // PER_HALF][:, SEQ * (b % PER_HALF):SEQ * (b % PER_HALF + 1)],
                       urep[:, b, :, :].rearrange("p a b -> p (a b)"), xT[:, SEQ * b:SEQ * (b + 1)])
                if b % PER_HALF == PER_HALF - 1:
                    m.then_inc(t_mm, 1)
            pe.wait_ge(wstack_done, 1)
            for u, (kind, half, i) in enumerate(UNITS):
                if u == 0 or UNITS[u - 1][1] != half:
                    pe.wait_ge(t_done, half + 1)
                if u >= len(PROJ_BANKS):
                    pe.wait_ge(*unit_free(u - len(PROJ_BANKS)))
                dst = bank[PROJ_BANKS[u % len(PROJ_BANKS)]]
                tokens = slice(half * HALF, (half + 1) * HALF)
                if kind == "k":
                    m = mm(dst[:], wst[:, 1, 128 * i:128 * (i + 1)], ts[:, tokens])
                elif kind == "v":
                    for b in range(BATCH):
                        m = mm(dst[:, 64 * b:64 * (b + 1)], ts[:, SEQ * b:SEQ * (b + 1)], wc[:, 128:192])
                else:
                    m = mm(dst[:], vst[:], ts[:, tokens])
                m.then_inc(proj_mm, 1)

            def queries(b):
                if b >= 2:
                    pe.wait_ge(q_done, b - 1)
                for G in range(GROUPS):
                    m = mm(bank[1 + b % 2][:, 128 * G:128 * (G + 1)], wst[:, 0, 128 * G:128 * (G + 1)],
                           ts[:, SEQ * b:SEQ * (b + 1)], start=G == 0, stop=False, skip_group_check=True)
                m.then_inc(q_mm, 1)

            def first_scores(b, r):
                if b >= 1:
                    pe.wait_ge(exp_done, 4 * (b - 1) + r + 1)
                rows = slice(32 * r, 32 * r + 8)
                for G in range(GROUPS):
                    m = mm(bank[3 + r][:, 128 * G:128 * (G + 1)], hi16[rows, b % 2, 128 * G:128 * (G + 1)],
                           kop[rows, G, SEQ * b:SEQ * (b + 1)], tile_position=(32 * r, 0))
                m.then_inc(s1_mm, 1)

            queries(0)
            for u in range(len(UNITS) - len(PROJ_BANKS), len(UNITS)):
                pe.wait_ge(*unit_free(u))
            pe.wait_ge(q_hi, 1)
            for r in range(4):
                first_scores(0, r)
            def minus_max(b):
                pe.wait_ge(mx_done, 4 * (b + 1))
                for G in range(GROUPS):
                    m = mm(bank[1 + b % 2][:, 128 * G:128 * (G + 1)], negm[:, b % 2, G, :], ident16[:],
                           start=False, stop=G == GROUPS - 1, skip_group_check=True)
                m.then_inc(negm_mm, 1)

            def sums(b, r):
                pe.wait_ge(exp_done, 4 * b + r + 1)
                for G in range(GROUPS):
                    cols = slice(128 * G, 128 * (G + 1))
                    h = 4 * G + r
                    mm(bank[7][32 * r:32 * r + 32, cols], val[:, b, 32 * h:32 * h + 32],
                       probs[:, b % 2, r, cols], tile_position=(0, 32 * r))
                    m = mm(bank[0][32 * r:32 * r + 32, cols], ones32[:],
                           probs[:, b % 2, r, cols], tile_position=(0, 32 * r))
                if r == 3:
                    m.then_inc(av_mm, 1)

            def output_projection(half):
                pe.wait_ge(ao_done, PER_HALF * (half + 1))
                for G in range(GROUPS):
                    a = CONST_AT["ow"][0] + D * G
                    m = mm(bank[1 + half][:], const[:, a:a + D], ao[:, G, half * HALF:(half + 1) * HALF],
                           start=G == 0, stop=G == GROUPS - 1)
                m.then_inc(mo_mm, 1)

            minus_max(0)
            for b in range(BATCH):
                if b + 1 < BATCH:
                    queries(b + 1)
                pe.wait_ge(q_done, b + 1)
                for r in range(4):
                    rows = slice(32 * r, 32 * r + 32)
                    for G in range(GROUPS):
                        m = mm(bank[3 + r][:, 128 * G:128 * (G + 1)], kop[rows, G, SEQ * b:SEQ * (b + 1)],
                               qop[rows, b % 2, 128 * G:128 * (G + 1)], tile_position=(32 * r, 0))
                    m.then_inc(s2_mm, 1)
                if b + 1 < BATCH:
                    pe.wait_ge(q_hi, b + 2)
                if b >= 1:
                    pe.wait_ge(ao_done, b)
                else:
                    pe.wait_ge(v_done, 1)
                for r in range(4):
                    if b + 1 < BATCH:
                        first_scores(b + 1, r)
                    if r == 1:
                        sums(b, 0)
                sums(b, 1)
                if b + 1 < BATCH:
                    minus_max(b + 1)
                else:
                    output_projection(0)
                sums(b, 2)
                sums(b, 3)
            output_projection(1)
            pe.wait_ge(wsq_done, 2)
            for w in range(2):
                m = mm(bank[3][:, 8 * w:8 * w + 8], wsq[:, w, :], style2[:, w, :])
            m.then_inc(demod_mm, 1)

            def route(layer):
                for half in range(HALVES):
                    if layer == 0:
                        pe.wait_ge(mo_done, half + 1)
                    else:
                        pe.wait_ge(mo_tile_read, PER_HALF * (half + 1))
                    if layer == 0 and half == 0:
                        pe.wait_ge(ao_done, BATCH)
                    for t in range(half * PER_HALF, (half + 1) * PER_HALF):
                        m = mm(bank[0][:, E * t:E * (t + 1)], mo[:, SEQ * t:SEQ * (t + 1)], C(f"rw{layer}"))
                m.then_inc(rt_mm, 1)
                if layer == 0:
                    pe.wait_ge(diag_done, 1)
                    for b in range(BATCH):
                        m = mm(bank[5 + b // PER_HALF][:, SEQ * (b % PER_HALF):SEQ * (b % PER_HALF + 1)],
                               C("wk"), diag[:, b, :])
                    m.then_inc(wmod_mm, 1)
                pe.wait_ge(parts_done, layer + 1)
                for half in range(HALVES):
                    for t in range(PER_HALF):
                        m = nc.tensor.transpose(bank[(0, 7)[half]][0:16, 128 * t:128 * (t + 1)],
                                                parts[:, half * PER_HALF + t, :].bitcast(F32), C("ident"))
                    m.then_inc(parts_tr, 1)
                if layer == 0:
                    for half in range(HALVES):
                        pe.wait_ge(comb_done, half + 1)
                        mm(bank[(0, 7)[half]][:], selp[:, E * 128:], comb_t[:, half, :].bitcast(F32)).then_inc(b2_mm, 1)

            def slots(k, first, count):
                base = weight_slot(k) + 128 * first
                return slice(base, base + 128 * count)

            def first_product(c):
                j, fc = CHUNK_LIST[c]
                layer, e, half = JOBS[j]
                k = layer * E + e
                if fc == 0:
                    if j >= 2:
                        pe.wait_ge(cb_read, j - 1)
                    mm(bank[5 + j % 2][:], sel[:, 128 * e:128 * (e + 1)], comb_t[:, half, :]).then_inc(cb_mm, 1)
                    pe.wait_ge(w_done, k + 1)
                if c >= 3:
                    pe.wait_ge(gelu_done, c - 2)
                tokens = slice(half * HALF, (half + 1) * HALF)
                at = slots(k, fc, 1)
                dst = bank[1 + c % 3][:]
                if layer == 0 and c < 2:
                    pe.wait_ge(mo_done, HALVES)
                mm(dst, w_hi[:, at], mo_hi[:, tokens], stop=False)
                mm(dst, w_hi[:, at], mo_lo[:, tokens], start=False, stop=False)
                mm(dst, w_lo[:, at], mo_hi[:, tokens], start=False).then_inc(h_mm, 1)

            def second_product(c):
                j, fc = CHUNK_LIST[c]
                layer, e, half = JOBS[j]
                k = layer * E + e
                n = CHUNKS[layer]
                if fc == 0 and j >= 2:
                    pe.wait_ge(weighted_done, j - 1)
                pe.wait_ge(lo_done, c + 1)
                at = slots(k, n + fc, 1)
                dst = bank[(4, 7)[j % 2]][:]
                mm(dst, w_hi[:, at], g_hi[:, c % 3, :], start=fc == 0, stop=False)
                mm(dst, w_hi[:, at], g_lo[:, c % 3, :], start=False, stop=False)
                mm(dst, w_lo[:, at], g_hi[:, c % 3, :], start=False, stop=fc == n - 1).then_inc(y_mm, 1)

            def experts(layer):
                first, end = FIRST_CHUNK[layer * JOBS_PER_LAYER], END_CHUNK[(layer + 1) * JOBS_PER_LAYER - 1]
                pe.wait_ge(mo_split, HALVES * (layer + 1))
                pe.wait_ge(comb_done, HALVES * (layer + 1))
                pe.wait_ge(wmod_done, 1)
                for c in range(first, end + LAG):
                    if c < end:
                        first_product(c)
                    if c - LAG >= first:
                        second_product(c - LAG)

            route(0)
            experts(0)

            for half in range(HALVES):
                pe.wait_ge(x1_done, half + 1)
                if half == 0:
                    pe.wait_ge(wmod_done, 1)
                for b in range(half * PER_HALF, (half + 1) * PER_HALF):
                    m = mm(bank[1 + half][:, SEQ * (b % PER_HALF):SEQ * (b % PER_HALF + 1)],
                           x1[:, SEQ * b:SEQ * (b + 1)], wmod[:, b, :])
                m.then_inc(kx_mm, 1)

            def output(b):
                pe.wait_ge(att_read, b + 1)
                if b >= 2:
                    pe.wait_ge(mo_tile_read, b - 1)
                mm(bank[5 + b % 2][:, 0:SEQ], C("wo_t"), att_t[:, b % 2, :]).then_inc(mo_tile, 1)

            for b in range(BATCH):
                if b >= 2:
                    pe.wait_ge(att_read, b - 1)
                pe.wait_ge(prod_near, b + 1)
                for s in range(H1):
                    if s == NEAR:
                        pe.wait_ge(prod_far, b + 1)
                    m = mm(bank[3 + b % 2][:, 0:128], prod[:, b % 2, 128 * s:128 * (s + 1)], C("ident"),
                           start=s == 0, stop=s == H1 - 1)
                m.then_inc(att_mm, 1)
                if b >= 1:
                    output(b - 1)
            output(BATCH - 1)
            route(1)
            experts(1)

        @block.scalar
        def _(act):
            def activate(dst, src, func, **kw):
                return nc.scalar.activation(dst, src, func, **kw)

            for b in range(BATCH):
                if b % PER_HALF == 0:
                    act.wait_ge(t_mm, b // PER_HALF + 1)
                activate(ts[:, SEQ * b:SEQ * (b + 1)],
                         bank[1 + b // PER_HALF][:, SEQ * (b % PER_HALF):SEQ * (b % PER_HALF + 1)],
                         ACT.Identity, bias=ubias[:, b:b + 1]).then_inc(t_hi, 1)
            nk = 0
            for u, (kind, half, i) in enumerate(UNITS):
                src = bank[PROJ_BANKS[u % len(PROJ_BANKS)]][:]
                if kind == "hs":
                    continue
                act.wait_ge(proj_mm, u + 1)
                if kind == "k":
                    if nk >= 2:
                        act.wait_ge(k_done, nk - 1)
                    activate(hi16[:, nk % 2, :], src, ACT.Copy).then_inc(k_hi, 1)
                    nk += 1
                else:
                    act.wait_ge(val_clear, 1)
                    activate(val[:].rearrange("p b (h c) -> p (b h) c", h=HEADS)[:, :, 0:KPH],
                             src.rearrange("p (n c) -> p n c", c=KPH), ACT.Copy).then_inc(v_done, 1)

            def query_parts(b):
                act.wait_ge(q_mm, b + 1)
                if b < 2:
                    act.wait_ge(k_done, GROUPS * HALVES)
                else:
                    act.wait_ge(q_done, b - 1)
                activate(hi16[:, b % 2, :], bank[1 + b % 2][:], ACT.Copy).then_inc(q_hi, 1)

            def inverse_sums(b):
                act.wait_ge(av_mm, b + 1)
                if b >= 1:
                    act.wait_ge(ao_done, b)
                activate(rz[:], bank[0][:], ACT.Ln).then_inc(log_done, 1)
                act.wait_ge(log_done, b + 1)
                activate(rz[:], rz[:], ACT.Exp, scale=-1.0).then_inc(inv_done, 1)

            nc.scalar.preload_act_table_set("natural_log_exp_and_others")
            query_parts(0)
            for b in range(BATCH):
                if b + 1 < BATCH:
                    query_parts(b + 1)
                if b >= 1:
                    inverse_sums(b - 1)
                for r in range(4):
                    act.wait_ge(s2_mm, 4 * b + r + 1)
                    if b >= 2 and r == 0:
                        act.wait_ge(av_mm, b - 1)
                    activate(probs[:, b % 2, r, :], bank[3 + r][:], ACT.Exp,
                             scale=float(KPH) ** -0.5).then_inc(exp_done, 1)

            inverse_sums(BATCH - 1)

            def soft(q):
                act.wait_ge(sub_done, q + 1)
                pair = amat[:, q % 2, :, :, :].rearrange("p t s h -> p (t s h)")
                activate(pair, pair, ACT.Exp, scale=float(D1) ** -0.5).then_inc(soft_exp, 1)

            def block_output(b):
                act.wait_ge(mo_tile, b + 1)
                activate(mo[:, SEQ * b:SEQ * (b + 1)], bank[5 + b % 2][:, 0:SEQ],
                         ACT.Identity, scale=demod[:, 1, b:b + 1], bias=C("ob1")).then_inc(mo_tile_read, 1)

            def routing(layer):
                act.wait_ge(rt_sub, layer + 1)
                activate(rt[:, 1, :, :], rt[:, 0, :, :], ACT.Exp).then_inc(rt_exp, 1)

            def experts(layer):
                for c in range(FIRST_CHUNK[layer * JOBS_PER_LAYER], END_CHUNK[(layer + 1) * JOBS_PER_LAYER - 1]):
                    j, fc = CHUNK_LIST[c]
                    _, e, half = JOBS[j]
                    act.wait_ge(h_mm, c + 1)
                    if c >= 3:
                        act.wait_ge(lo_done, c - 2)
                    if layer == 0:
                        a = CONST_AT["b1"][0] + CHUNKS[0] * e + fc
                        activate(g[:, c % 3, :], bank[1 + c % 3][:], ACT.Gelu, bias=const[:, a:a + 1]).then_inc(gelu_done, 1)
                    else:
                        activate(g[:, c % 3, :], bank[1 + c % 3][:], ACT.Gelu).then_inc(gelu_done, 1)
                    act.wait_ge(gelu_done, c + 1)
                    if c >= 3:
                        act.wait_ge(y_mm, c - 2)
                    activate(g_hi[:, c % 3, :], g[:, c % 3, :], ACT.Copy).then_inc(hi_done, 1)
                    if fc == 0:
                        act.wait_ge(cb_mm, j + 1)
                        if j >= 2:
                            act.wait_ge(weighted_done, j - 1)
                        activate(cbs[:, j % 2, :], bank[5 + j % 2][:], ACT.Copy).then_inc(cb_read, 1)

            for half in range(HALVES):
                act.wait_ge(mo_mm, half + 1)
                activate(mo[:, half * HALF:(half + 1) * HALF], bank[1 + half][:], ACT.Identity,
                         bias=C("ob0")).then_inc(mo_done, 1)
            act.wait_ge(demod_mm, 1)
            activate(demod[:].rearrange("p w b -> p (w b)"), bank[3][:, 0:2 * BATCH], ACT.Sqrt, bias=eps[:]).then_inc(demod_read, 1)
            routing(0)
            act.wait_ge(wmod_mm, 1)
            for b in range(BATCH):
                ins = activate(wmod[:, b, :], bank[5 + b // PER_HALF][:, SEQ * (b % PER_HALF):SEQ * (b % PER_HALF + 1)],
                               ACT.Copy, scale=style[:, 0, b:b + 1])
            ins.then_inc(wmod_done, 1)
            experts(0)

            for half in range(HALVES):
                act.wait_ge(kx_done, half + 1)
                rows = kx2[:, half * PER_HALF:(half + 1) * PER_HALF, :]
                activate(rows[:, :, 128:256], rows[:, :, 0:128], ACT.Copy).then_inc(kx_dup, 1)
                if half == 0:
                    soft(0)
            for b in range(BATCH):
                if b % 2 == 0 and b + 2 < BATCH:
                    soft(b // 2 + 1)
                act.wait_ge(att_mm, b + 1)
                if b >= 2:
                    act.wait_ge(mo_tile, b - 1)
                activate(att_t[:, b % 2, :], bank[3 + b % 2][:, 0:128], ACT.Copy,
                         scale=style[:, 1, b:b + 1]).then_inc(att_read, 1)
                if b >= 1:
                    block_output(b - 1)
            block_output(BATCH - 1)
            routing(1)
            experts(1)

        @block.vector
        def _(dve):
            v = nc.vector
            linked = [0]

            def link(ins):
                ins.then_inc(dve_chain, 1)
                linked[0] += 1
                dve.wait_ge(dve_chain, linked[0])

            v.memset(urep[:], 0.0)
            v.memset(negm[:], 0.0)
            v.memset(ones32[:], 1.0)
            link(v.memset(wst[:].bitcast(F32), 0.0))
            dve.wait_ge(u_mm, 1)
            for blk in range(4):
                v.tensor_copy(urep[:, :, blk, 0:RANK], view(bank[0], 0, [[1, BATCH], [8, RANK]]))
            v.tensor_copy(ubias[:], bank[0][:, 240:248])
            link(v.tensor_copy(style[:].rearrange("p w b -> p (w b)"), bank[0][:, 248:264]))
            v.tensor_tensor(style2[:], style[:], style[:], ALU.mult).then_inc(u_done, 1)
            dve.wait_ge(ld_proj, 16)
            dve.wait_ge(wstack_mm, 1)
            link(v.tensor_tensor(wfull[:], bank[3][:, 0:QKV], PP("bias"), ALU.add))
            v.tensor_copy(wc[:], wfull[:])
            link(v.tensor_copy(vst[:], PP("vrep")))
            for rows in (slice(32, 64), slice(96, 128)):
                v.tensor_tensor(vst[rows, :], PP("vrep")[rows, :], vst[rows, :].bitcast(F32), ALU.subtract)
                ins = v.tensor_tensor(wc[rows, :], wfull[rows, :], wc[rows, :].bitcast(F32), ALU.subtract)
            link(ins)
            for w in range(2):
                v.tensor_copy(view(wst[:, w, :], 0, [[32, HEADS], [4, 4], [1, KPH]]),
                              view(wc[:], 64 * w, [[KPH, HEADS], [0, 4], [1, KPH]]).bitcast(F32))
            v.tensor_copy(view(wst[:, 1, :], 16, [[32, HEADS]]), PP("one").to_broadcast([128, HEADS])).then_inc(wstack_done, 1)
            for b in range(BATCH):
                dve.wait_ge(t_hi, PER_HALF * (b // PER_HALF + 1))
                cols = slice(SEQ * b, SEQ * (b + 1))
                ins = v.scalar_tensor_tensor(
                    ts[64:128, cols], bank[1 + b // PER_HALF][64:128, SEQ * (b % PER_HALF):SEQ * (b % PER_HALF + 1)],
                    ubias[64:128, b:b + 1], ts[64:128, cols].bitcast(F32), ALU.add, ALU.subtract)
                if b % PER_HALF == PER_HALF - 1:
                    ins.then_inc(t_done, 1)
            nk = 0
            for u, (kind, half, i) in enumerate(UNITS):
                src = bank[PROJ_BANKS[u % len(PROJ_BANKS)]][:]
                tokens = slice(half * HALF, (half + 1) * HALF)
                if kind == "k":
                    nk += 1
                    dve.wait_ge(k_hi, nk)
                    v.scalar_tensor_tensor(kop[:, i, tokens], hi16[:, (nk - 1) % 2, :], PP("mk"), src,
                                           ALU.mult, ALU.add).then_inc(k_done, 1)
                elif kind == "hs":
                    dve.wait_ge(proj_mm, u + 1)
                    v.tensor_tensor(xhs[:, tokens], src, xT[:, tokens], ALU.add).then_inc(hs_done, 1)
            dve.wait_ge(ld_const, 32)
            v.memset(eps[:], DEMOD_EPS)
            v.tensor_copy(sel[:], selp[:, 0:E * 128])
            v.tensor_copy(ident16[:], C("ident")).then_inc(consts_made, 1)

            def normalise(b):
                dve.wait_ge(inv_done, b + 1)
                link(v.tensor_tensor(newton[:], bank[0][:], rz[:], ALU.mult))
                link(v.scalar_tensor_tensor(newton[:], newton[:], 2.0, rz[:], ALU.subtract, ALU.mult))
                v.scalar_tensor_tensor(ao[:, :, SEQ * b:SEQ * (b + 1)], bank[7][:].rearrange("p (g s) -> p g s", g=GROUPS),
                                       -1.0, newton[:].rearrange("p (g s) -> p g s", g=GROUPS),
                                       ALU.mult, ALU.mult).then_inc(ao_done, 1)

            for b in range(BATCH):
                for r in range(4):
                    dve.wait_ge(s1_mm, 4 * b + r + 1)
                    if b >= 2 and r == 0:
                        dve.wait_ge(negm_mm, b - 1)
                    v.tensor_reduce(negm[:, b % 2, :, 32 * r + 16:32 * r + 17],
                                    bank[3 + r][:].rearrange("p (g t) -> p g t", g=GROUPS),
                                    AX.X, ALU.max, negate=True).then_inc(mx_done, 1)
                dve.wait_ge(negm_mm, b + 1)
                dve.wait_ge(q_hi, b + 1)
                v.scalar_tensor_tensor(qop[:, b % 2, :], hi16[:, b % 2, :], PP("mq"), bank[1 + b % 2][:],
                                       ALU.mult, ALU.add).then_inc(q_done, 1)
                if b >= 1:
                    normalise(b - 1)
            normalise(BATCH - 1)
            dve.wait_ge(demod_read, 1)
            link(v.reciprocal(demod[:], demod[:]))
            for b in range(BATCH):
                ins = v.tensor_scalar(diag[:, b, :], C("ident"), demod[:, 0, b:b + 1], None, ALU.mult)
            ins.then_inc(diag_done, 1)

            def split_output(layer):
                for half in range(HALVES):
                    tokens = slice(half * HALF, (half + 1) * HALF)
                    if layer == 0:
                        dve.wait_ge(mo_done, half + 1)
                    else:
                        dve.wait_ge(mo_tile_read, PER_HALF * (half + 1))
                    link(v.tensor_copy(mo_hi[:, tokens], mo[:, tokens]))
                    v.tensor_tensor(mo_lo[:, tokens], mo[:, tokens], mo_hi[:, tokens].bitcast(F32),
                                    ALU.subtract).then_inc(mo_split, 1)

            def routing(layer):
                wide = [128, BATCH, E]
                logits, p, one, key, two, rest = (rt[:, i, :, :] for i in (2, 1, 3, 4, 5, 6))
                top, inv, most, second, total = (rs[:, i, :, :] for i in (0, 1, 2, 3, 4))
                src = bank[0][:, 0:BATCH * E].rearrange("p (t e) -> p t e", t=BATCH)
                rank = C("rank").rearrange("p (t e) -> p t e", t=BATCH)

                def pick(dst, values, largest):
                    link(v.tensor_tensor(key, values, largest.to_broadcast(wide), ALU.is_equal))
                    link(v.tensor_tensor(key, key, rank, ALU.mult))
                    link(v.tensor_reduce(most, key, AX.X, ALU.max))
                    link(v.tensor_tensor(dst, key, most.to_broadcast(wide), ALU.is_equal))

                dve.wait_ge(rt_mm, layer + 1)
                if layer == 0:
                    link(v.tensor_tensor(logits, src, C("rb").rearrange("p (t e) -> p t e", t=BATCH), ALU.add))
                else:
                    link(v.tensor_copy(logits, src))
                link(v.tensor_reduce(top, logits, AX.X, ALU.max))
                v.tensor_tensor(rt[:, 0, :, :], logits, top.to_broadcast(wide), ALU.subtract).then_inc(rt_sub, 1)
                dve.wait_ge(rt_exp, layer + 1)
                link(v.tensor_reduce(total, p, AX.X, ALU.add))
                link(v.tensor_reduce(top, p, AX.X, ALU.max))
                pick(one, p, top)
                link(v.scalar_tensor_tensor(rest, one, -2.0, p, ALU.mult, ALU.add))
                link(v.tensor_reduce(second, rest, AX.X, ALU.max))
                pick(two, rest, second)
                link(v.tensor_tensor(one, one, two, ALU.add))
                v.tensor_tensor(one, one, p, ALU.mult)
                link(v.tensor_tensor(inv, top, second, ALU.add))
                if layer == 0:
                    link(v.scalar_tensor_tensor(inv, total, TOP_EPS, inv, ALU.mult, ALU.add))
                link(v.reciprocal(inv, inv))
                link(v.tensor_tensor(one, one, inv.to_broadcast(wide), ALU.mult))
                link(v.tensor_copy(parts[:, :, 0:E], one))
                v.tensor_tensor(parts[:, :, E:2 * E], one, parts[:, :, 0:E].bitcast(F32),
                                ALU.subtract).then_inc(parts_done, 1)
                for half in range(HALVES):
                    dve.wait_ge(parts_tr, layer * HALVES + half + 1)
                    v.tensor_copy(comb_t[:, half, :], bank[(0, 7)[half]][0:16, :]).then_inc(comb_done, 1)
                if layer == 0:
                    for half in range(HALVES):
                        dve.wait_ge(b2_mm, half + 1)
                        v.tensor_copy(acc[:, half * HALF:(half + 1) * HALF], bank[(0, 7)[half]][:]).then_inc(acc_init, 1)

            def weigh(j):
                dve.wait_ge(y_mm, END_CHUNK[j])
                dve.wait_ge(cb_read, j + 1)
                if j >= 2:
                    dve.wait_ge(acc_done, j - 1)
                v.tensor_tensor(weighted[:, j % 2, :], bank[(4, 7)[j % 2]][:], cbs[:, j % 2, :],
                                ALU.mult).then_inc(weighted_done, 1)

            def experts(layer):
                first, end = FIRST_CHUNK[layer * JOBS_PER_LAYER], END_CHUNK[(layer + 1) * JOBS_PER_LAYER - 1]
                for c in range(first, end + LAG):
                    if c < end:
                        dve.wait_ge(hi_done, c + 1)
                        if c >= 3:
                            dve.wait_ge(y_mm, c - 2)
                        v.tensor_tensor(g_lo[:, c % 3, :], g[:, c % 3, :], g_hi[:, c % 3, :].bitcast(F32),
                                        ALU.subtract).then_inc(lo_done, 1)
                    d = c - LAG
                    if first <= d and END_CHUNK[CHUNK_LIST[d][0]] == d + 1:
                        weigh(CHUNK_LIST[d][0])

            split_output(0)
            routing(0)
            experts(0)
            for half in range(HALVES):
                tokens = slice(half * HALF, (half + 1) * HALF)
                dve.wait_ge(acc_done, JOBS_PER_LAYER)
                v.scalar_tensor_tensor(x1[:, tokens], acc[:, tokens], MOE_SCALE, xhs[:, tokens],
                                       ALU.mult, ALU.add).then_inc(x1_done, 1)

            def keys(half):
                dve.wait_ge(kx_mm, half + 1)
                v.tensor_tensor(kx2[:, half * PER_HALF:(half + 1) * PER_HALF, 0:128],
                                bank[1 + half][:].rearrange("p (t c) -> p t c", t=PER_HALF),
                                view(C("kb"), 0, [[0, PER_HALF], [1, 128]]), ALU.add).then_inc(kx_done, 1)

            def scores(q):
                i = q % 2
                pair = kx2[:, 2 * q:2 * q + 2, :]
                dve.wait_ge(kx_dup, q // 2 + 1)
                link(v.tensor_tensor(dots.rearrange("p (t s c) -> p t s c", t=2, s=NEAR),
                                     view(pair, 0, [[256, 2], [0, NEAR], [1, 128]]),
                                     view(pair, 0, [[256, 2], [D1, NEAR], [1, 128]]), ALU.mult))
                link(v.tensor_reduce(gram[:, :, 0:NEAR, 0:H1],
                                     dots.rearrange("p (t s h d) -> p t s h d", t=2, s=NEAR, h=H1), AX.X, ALU.add))
                link(v.tensor_copy(gram[:, :, 1:H1 // 2, H1:2 * H1], gram[:, :, 1:H1 // 2, 0:H1]))
                link(v.tensor_copy(gram[:, :, NEAR:H1, 0:H1],
                                   view(gram[:], 2 * H1 + H1 - 1, [[2 * H1 * H1, 2], [2 * H1 - 1, H1 // 2 - 1], [1, H1]])))
                link(v.tensor_reduce(small[:, i, 0, :, :], gram[:, :, :, 0:H1].rearrange("p t s h -> p t h s"),
                                     AX.X, ALU.max))
                if q >= 2:
                    dve.wait_ge(prod_far, 2 * q - 2)
                v.tensor_tensor(amat[:, i, :, :, :], gram[:, :, :, 0:H1],
                                view(small[:, i, 0, :, :], 0, [[H1, 2], [0, H1], [1, H1]]),
                                ALU.subtract).then_inc(sub_done, 1)

            def weights(q):
                i = q % 2
                dve.wait_ge(soft_exp, q + 1)
                link(v.tensor_reduce(small[:, i, 1, :, :], amat[:, i, :, :, :].rearrange("p t s h -> p t h s"),
                                     AX.X, ALU.add))
                link(v.reciprocal(small[:, i, 1, :, :], small[:, i, 1, :, :]))
                v.tensor_tensor(amat[:, i, :, :, :], amat[:, i, :, :, :],
                                view(small[:, i, 1, :, :], 0, [[H1, 2], [0, H1], [1, H1]]), ALU.mult).then_inc(a_done, 1)
                dve.wait_ge(a_done, q + 1)
                for b in (2 * q, 2 * q + 1):
                    if b >= 2:
                        dve.wait_ge(att_mm, b - 1)
                    v.tensor_tensor(prod[:, b % 2, 0:NEAR * 128].rearrange("p (s h d) -> p s h d", s=NEAR, h=H1),
                                    view(amat[:, i, b % 2, :, :], 0, [[H1, NEAR], [1, H1], [0, D1]]),
                                    view(kx2[:, b, :], 0, [[D1, NEAR], [D1, H1], [1, D1]]), ALU.mult).then_inc(prod_near, 1)

            keys(0)
            scores(0)
            keys(1)
            for q in range(BATCH // 2):
                if q + 1 < BATCH // 2:
                    scores(q + 1)
                weights(q)
            split_output(1)
            routing(1)
            experts(1)
            for half in range(HALVES):
                tokens = slice(half * HALF, (half + 1) * HALF)
                dve.wait_ge(acc_done, 2 * JOBS_PER_LAYER)
                v.tensor_tensor(xhs[:, tokens], acc[:, tokens], x1[:, tokens], ALU.add).then_inc(out_done, 1)

        @block.gpsimd
        def _(pool):
            p = nc.gpsimd

            p.memset(val[:], 0.0).then_inc(val_clear, 1)

            def split_weights(k):
                if k >= 2 * E:
                    return
                width = 2 * CHUNKS[k // E] * 128
                pool.wait_ge(ld_w[k % 2], 16 * (k // 2 + 1))
                if slot_free(k) is not None:
                    pool.wait_ge(y_mm, END_CHUNK[slot_free(k) * HALVES + HALVES - 1])
                at = slice(weight_slot(k), weight_slot(k) + width)
                p.tensor_copy(w_hi[:, at], raw[:, k % 2, 0:width]).then_inc(pool_chain, 1)
                pool.wait_ge(pool_chain, k + 1)
                p.tensor_tensor(w_lo[:, at], raw[:, k % 2, 0:width], w_hi[:, at].bitcast(F32),
                                ALU.subtract).then_inc(w_done, 1)

            def accumulate(j):
                half = JOBS[j][2]
                tokens = slice(half * HALF, (half + 1) * HALF)
                pool.wait_ge(weighted_done, j + 1)
                if j >= 1:
                    pool.wait_ge(acc_done, j)
                p.tensor_tensor(acc[:, tokens], acc[:, tokens], weighted[:, j % 2, :], ALU.add).then_inc(acc_done, 1)

            def layer_of_experts(layer):
                for e in range(E):
                    k = layer * E + e
                    if layer == 0 and e in (1, 2, 4, 6):
                        split_weights({1: 6, 2: 7, 4: 8, 6: 9}[e])
                    elif layer == 1:
                        split_weights(k + 2)
                    for half in range(HALVES):
                        accumulate(k * HALVES + half)

            for k in range(6):
                split_weights(k)
                if k == 0:
                    pool.wait_ge(ld_const, 32)
                    for w, name in enumerate(("wk_t", "wo_t")):
                        p.tensor_tensor(wsq[:, w, :], C(name), C(name), ALU.mult).then_inc(wsq_done, 1)
            pool.wait_ge(acc_init, HALVES)
            layer_of_experts(0)
            pool.wait_ge(x1_done, HALVES)
            p.memset(acc[:], 0.0).then_inc(acc_zero, 1)
            for b in range(BATCH):
                i = b % 2
                pool.wait_ge(a_done, b // 2 + 1)
                if b >= 2:
                    pool.wait_ge(att_mm, b - 1)
                p.tensor_tensor(prod[:, i, NEAR * 128:].rearrange("p (s h d) -> p s h d", s=H1 - NEAR, h=H1),
                                view(amat[:, b // 2 % 2, b % 2, :, :], H1 * NEAR, [[H1, H1 - NEAR], [1, H1], [0, D1]]),
                                view(kx2[:, b, :], D1 * (H1 - 1), [[-D1, H1 - NEAR], [D1, H1], [1, D1]]),
                                ALU.mult).then_inc(prod_far, 1)
            pool.wait_ge(acc_zero, 1)
            layer_of_experts(1)


def kernel(**inputs):
    import numpy as np
    import concourse.bacc as bacc
    from concourse.bass_utils import run_bass_kernel_spmd

    t = {k: np.asarray(v) for k, v in inputs.items()}
    f32 = np.float32

    cond = np.ones((COND + 1, BATCH), f32)
    cond[:COND] = t["cond_512"].T
    wdec = np.concatenate([t["L0_cond_W_dec"], t["L0_cond_b_dec"][None]], 0).reshape(COND + 1, D + 1, RANK)
    ubias = np.zeros((COND + 1, 4, 32), f32)
    ubias[:, :, :RANK] = wdec[:, D, None, :]
    ubias[COND, :, RANK] = 1.0
    kaff = np.concatenate([t["L1_cond_k_aff_w"].T, t["L1_cond_k_aff_b"][None]], 0)
    oaff = np.concatenate([t["L1_cond_o_aff_w"].T, t["L1_cond_o_aff_b"][None]], 0)
    cond_pack = np.concatenate([wdec[:, :D].transpose(0, 2, 1).reshape(COND + 1, RANK * D),
                                ubias.reshape(COND + 1, 128), cond, kaff, oaff], 1)

    V = t["L0_cond_V"]
    vrep = np.zeros((4, 32, D), f32)
    vrep[:, :RANK] = V[None]
    vrep = vrep.reshape(128, D)
    def first_columns(q):
        return q.reshape(-1, HEADS, 2 * KPH)[:, :, :KPH].reshape(-1, HEADS * KPH)

    w_qkv = np.concatenate([first_columns(t["L0_ffn_q_w"]), t["L0_ffn_k_w"], t["L0_ffn_v_w"]], 1)
    bias = np.zeros((4, 32, QKV), f32)
    bias[:, RANK] = np.concatenate([first_columns(t["L0_ffn_q_b"][None]), t["L0_ffn_k_b"][None], t["L0_ffn_v_b"][None]], 1)
    row = np.arange(128) % 32
    mq = np.where((row >= 8) & (row < 16), -1.0, 0.0).astype(f32)[:, None]
    mk = np.where((row < 16) & (row % 8 >= 4), -1.0, 0.0).astype(f32)[:, None]
    one = np.zeros((128, 1), f32)
    one[RANK] = 1.0
    proj_pack = np.concatenate([vrep.T, w_qkv, bias.reshape(128, QKV), one, mq, mk, vrep], 1)

    ow = np.zeros((4, 32, GROUPS, D), f32)
    for G in range(GROUPS):
        for r in range(4):
            h = 4 * G + r
            ow[r, :4, G] = t["L0_ffn_o_w"][4 * h:4 * h + 4]
    rank = np.tile(np.arange(E, 0, -1).astype(f32), (128, BATCH))
    const_pack = np.concatenate([
        np.eye(128, dtype=f32), t["L1_cond_k_w"], t["L1_cond_k_w"].T, t["L1_cond_o_w"].T,
        np.tile(t["L1_cond_k_b"], (128, 1)), ow.reshape(128, GROUPS * D),
        t["L0_ffn_router_w"], t["L1_ffn_router_w"].T, np.tile(t["L0_ffn_router_b"], (128, BATCH)), rank,
        t["L0_ffn_b1"].reshape(E * CHUNKS[0], 128).T, t["L0_ffn_o_b"][:, None], t["L1_cond_o_b"][:, None]], 1)
    sel = np.zeros((2, E, E, 128), f32)
    for e in range(E):
        sel[:, e, e] = 1.0
    sel_pack = np.concatenate([sel.reshape(16, E * 128), np.tile(t["L0_ffn_b2"], (2, 1))], 1)

    def expert_weights(w1, w2, chunks):
        return np.concatenate([w1.transpose(1, 0, 2), w2.reshape(E, chunks, 128, D).transpose(2, 0, 1, 3)
                               .reshape(128, E, chunks * D)], 2)

    arrays = {
        "cond_pack": cond_pack, "proj_pack": proj_pack, "x_t": t["x"].reshape(TOK, D).T,
        "const_pack": const_pack, "sel_pack": sel_pack,
        "w_layer0": expert_weights(t["L0_ffn_w1"], t["L0_ffn_w2"], CHUNKS[0]),
        "w_layer1": expert_weights(t["L1_ffn_w1"], t["L1_ffn_w2"], CHUNKS[1]),
    }
    nc = bacc.Bacc("TRN2", target_bir_lowering=False, num_devices=1)
    feed, args = {}, []
    for name, a in arrays.items():
        a = np.ascontiguousarray(a)
        feed[f"in_{name}"] = a
        args.append(nc.dram_tensor(f"in_{name}", a.shape, mybir.dt.from_np(a.dtype), kind="ExternalInput").ap())
    args.append(nc.dram_tensor("out_t", (D, TOK), F32, kind="ExternalOutput").ap())
    program(nc, *args)
    r = run_bass_kernel_spmd(nc, [feed], core_ids=[0])
    return np.ascontiguousarray(r.results[0]["out_t"].T).reshape(BATCH, SEQ, D)
```

```python
from contextlib import ExitStack

import concourse.bass as bass
from concourse import mybir

BATCH, SEQ, D = 8, 128, 128
TOK = BATCH * SEQ
HALF = 512
HALVES = TOK // HALF
PER_HALF = HALF // SEQ
COND = 64
RANK = 30
HEADS, KPH = 16, 4
GROUPS = HEADS // 4
E = 8
CHUNKS = (256 // 128, 512 // 128)
H1, D1 = 16, D // 16
NEAR = H1 // 2 + 1
MOE_SCALE = 0.3
DEMOD_EPS = 1e-8
TOP_EPS = 1e-8

F32 = mybir.dt.float32
FR = mybir.dt.float32r
F16 = mybir.dt.float16
ALU = mybir.AluOpType
ACT = mybir.ActivationFunctionType
AX = mybir.AxisListType


def columns(*fields):
    at, found = 0, {}
    for name, width in fields:
        found[name] = (at, at + width)
        at += width
    return found, at


ROWS = 32
COND_AT, COND_W = columns(("cond", ROWS), ("ubias", 128), ("kaff", D), ("oaff", D), ("wdec", ROWS * D))
QKV = 3 * HEADS * KPH
PROJ_AT, PROJ_W = columns(("vt", 128), ("w", QKV), ("bias", QKV), ("one", 1), ("mq", 1), ("mk", 1), ("vrep", 128), ("ident", 128), ("spread", 128))
CONST_AT, CONST_W = columns(
    ("ident", 128), ("wk", D), ("wk_t", D), ("wo_t", D), ("kb", D), ("ow", D), ("rw0", E), ("rw1", E),
    ("rb", BATCH * E), ("rank", BATCH * E), ("b1", E * CHUNKS[0]), ("b2", E), ("ob0", 1), ("ob1", 1))

JOBS = [(layer, e, half) for layer in range(2) for e in range(E) for half in range(HALVES)]
CHUNK_LIST = [(j, fc) for j, (layer, _, _) in enumerate(JOBS) for fc in range(CHUNKS[layer])]
FIRST_CHUNK = {j: c for c, (j, fc) in enumerate(CHUNK_LIST) if fc == 0}
END_CHUNK = {j: c + 1 for c, (j, fc) in enumerate(CHUNK_LIST)}
JOBS_PER_LAYER = E * HALVES
WARM_UP = 12
LOGIT_BANK = (6, 7)
ROUTE_AFTER = (5, 8)
WMOD_AFTER = (20, 24)
MAX_AFTER = 1
NEAR_SLOTS = list(range(NEAR))
FAR_LEFT = list(range(NEAR, NEAR + 3)) + list(range(NEAR + 6, H1))
START_FILL = (1, 4)
FOLDED = BATCH - 3
LAG = 2


def program(nc, cond_pack, proj_pack, x_t, const_pack, sel_pack, w_layer0, w_layer1, out):
    with ExitStack() as ctx:
        def sb(name, shape, dt=F32):
            return ctx.enter_context(nc.sbuf_tensor(name, shape, dt))

        def sem(name):
            return ctx.enter_context(nc.semaphore(name))

        bank = [ctx.enter_context(nc.psum_tensor(f"bank{i}", [128, 512], F32)) for i in range(8)]

        early = sb("early", [128, COND_W])
        condp = early[0:COND + 1, :]
        ao = early[:, 0:TOK]
        projp = sb("projp", [128, PROJ_W])
        cbs = sb("cbs", [128, 2, 512])
        xT = sb("xT", [128, TOK])
        const = sb("const", [128, CONST_W])
        selp = sb("selp", [16, E * 128])
        raw = sb("raw", [128, 2, 1024])

        def C(name):
            a, b = CONST_AT[name]
            return const[:, a:b]

        def PP(name):
            a, b = PROJ_AT[name]
            return projp[:, a:b]

        def CP(name):
            a, b = COND_AT[name]
            return condp[:, a:b]

        zeros = sb("zeros", [128, 512], F16)
        eps = sb("eps", [128, 1])
        ident16 = sb("ident16", [128, 128], F16)
        sel = sb("sel", [16, E * 128], FR)
        probs = sb("probs", [128, 2, 4, 512])
        urows = probs[:, 0, 0:2, :].rearrange("p a b -> p (a b)")
        urep = sb("urep", [128, BATCH, 4, ROWS])
        ubias = sb("ubias", [128, 8])
        wfull = sb("wfull", [128, QKV])
        wc = sb("wc", [128, QKV], FR)
        wst = sb("wst", [128, 2, 512], FR)
        vst = sb("vst", [128, 128], FR)
        ts = sb("ts", [128, TOK], FR)
        hi16 = sb("hi16", [128, 2, 512], F16)
        kop = sb("kop", [128, GROUPS, TOK], F16)
        val = sb("val", [128, BATCH, 512])
        qop = sb("qop", [128, 2, 512], F16)
        negm = sb("negm", [128, 2, GROUPS, 128], F16)
        av = sb("av", [128, 2, SEQ])
        rz = sb("rz", [128, SEQ])
        newton = sb("newton", [128, SEQ])
        xhs = sb("xhs", [128, TOK])
        mo = sb("mo", [128, TOK])
        mo_hi = sb("mo_hi", [128, TOK], FR)
        mo_lo = sb("mo_lo", [128, TOK], FR)
        w_hi = sb("w_hi", [128, 3 * 1024], FR)
        w_lo = sb("w_lo", [128, 3 * 1024], FR)
        g_hi = sb("g_hi", [128, 3, 512], FR)
        g_lo = sb("g_lo", [128, 3, 512], FR)
        weighted = sb("weighted", [128, 2, 512])
        x1 = sb("x1", [128, TOK])
        rt = sb("rt", [128, 8, BATCH, E])
        rs = sb("rs", [128, 8, BATCH, 1])
        parts = sb("parts", [128, BATCH, 2 * E], FR)
        comb_t = sb("comb_t", [16, HALVES, HALF], FR)
        style = sb("style", [128, 2, BATCH])
        style2 = sb("style2", [128, 2, BATCH])
        wsq = sb("wsq", [128, 2, D])
        demod_step = sb("demod_step", [128, 2 * BATCH])
        demod = sb("demod", [128, 2, BATCH])
        wmod = sb("wmod", [128, BATCH, D])
        kx2 = val[:, 0:4, :].rearrange("p a b -> p (a b)").rearrange("p (b c) -> p b c", b=BATCH)
        gram = val[:, 4:6, :].rearrange("p t (s h) -> p t s h", s=H1)
        amat = val[:, 6:8, :].rearrange("p i (t s h) -> p i t s h", t=2, s=H1)
        dots = early[:, 0:2 * NEAR * D]
        att_t = early[:, 2 * NEAR * D:2 * NEAR * D + 2 * SEQ].rearrange("p (i c) -> p i c", i=2)
        diag = urep[:].rearrange("p b a r -> p b (a r)")
        prod = probs[:, :, :, :].rearrange("p i a b -> p i (a b)")
        small = sb("small", [128, 2, 2, 2, H1])

        def view(t, first, dims):
            a = t[:, ...] if not isinstance(t, bass.AP) else t
            return bass.AP(tensor=a.tensor, offset=a.offset + first, ap=[list(a.ap[0]), *[list(x) for x in dims]])

        def u_copy(blk, n):
            return (urep[:, :, blk, :].rearrange("p b (c k) -> p b c k", c=4)[:, :, :, 4 * n:4 * n + 4],
                    view(bank[4 + n], 0, [[1, BATCH], [32, 4], [128, 4]]))

        ld_proj, ld_cond, ld_x, ld_const = sem("ld_proj"), sem("ld_cond"), sem("ld_x"), sem("ld_const")
        ld_w = [sem("ld_w_even"), sem("ld_w_odd")]
        stored = sem("stored")
        zeros_made, sel_done = sem("zeros_made"), sem("sel_done")
        wstack_mm, wstack_done = sem("wstack_mm"), sem("wstack_done")
        u_mm, u_rows, u_tr, u_done, u_copied = sem("u_mm"), sem("u_rows"), sem("u_tr"), sem("u_done"), sem("u_copied")
        style_mm, ubias_done, style_done = sem("style_mm"), sem("ubias_done"), sem("style_done")
        demod_mm, demod_log, demod_read, demod_done, diag_done = (
            sem("demod_mm"), sem("demod_log"), sem("demod_read"), sem("demod_done"), sem("diag_done"))
        wmod_mm, wmod_done, wsq_done = sem("wmod_mm"), sem("wmod_done"), sem("wsq_done")
        val_zero, val_clear, av_read, sums_mm = sem("val_zero"), sem("val_clear"), sem("av_read"), sem("sums_mm")
        t_mm, t_hi, t_done = sem("t_mm"), sem("t_hi"), sem("t_done")
        proj_mm, k_hi, k_done, v_done, hs_done = sem("proj_mm"), sem("k_hi"), sem("k_done"), sem("v_done"), sem("hs_done")
        q_mm, q_hi, s1_mm, mx_done = sem("q_mm"), sem("q_hi"), sem("s1_mm"), sem("mx_done")
        negm_mm, q_done, s2_mm, exp_done = sem("negm_mm"), sem("q_done"), sem("s2_mm"), sem("exp_done")
        av_mm, log_done, inv_done, ao_done = sem("av_mm"), sem("log_done"), sem("inv_done"), sem("ao_done")
        mo_mm, mo_done, mo_split = sem("mo_mm"), sem("mo_done"), sem("mo_split")
        rt_mm, rt_sub, rt_exp, parts_done = sem("rt_mm"), sem("rt_sub"), sem("rt_exp"), sem("parts_done")
        parts_tr, comb_done = sem("parts_tr"), sem("comb_done")
        w_done, h_mm, gelu_done, lo_done, y_mm = (
            sem("w_done"), sem("h_mm"), sem("gelu_done"), sem("lo_done"), sem("y_mm"))
        cb_mm, cb_read, weighted_done, acc_done, x1_done = (
            sem("cb_mm"), sem("cb_read"), sem("weighted_done"), sem("acc_done"), sem("x1_done"))
        kx_dup, far_sum, near_sum = sem("kx_dup"), sem("far_sum"), sem("near_sum")
        kx_mm, kx_done, sub_done, soft_exp, a_done, prod_near, prod_far = (
            sem("kx_mm"), sem("kx_done"), sem("sub_done"), sem("soft_exp"), sem("a_done"), sem("prod_near"), sem("prod_far"))
        att_mm, att_read = sem("att_mm"), sem("att_read")
        dve_chain, pool_chain = sem("dve_chain"), sem("pool_chain")

        block = ctx.enter_context(nc.Block())

        def weight_slot(k):
            return 512 * (k % 6) if k < E else 1024 * ((k - E + 1) % 3)

        def by_gpsimd(j):
            return j % JOBS_PER_LAYER < JOBS_PER_LAYER - HALVES

        def accumulated(j):
            return j + 1 - HALVES * (j // JOBS_PER_LAYER)

        def slot_free(k):
            if k < E:
                return k - 6 if k >= 6 else None
            return {0: 3, 1: 5, 2: 7}.get(k - E, k - 3)

        UNITS = [(kind, half, i) for half in range(HALVES)
                 for kind, n in (("k", GROUPS), ("v", half), ("hs", 1)) for i in range(n)]
        PROJ_BANKS = [3, 4, 5, 6, 7]

        def unit_free(u):
            kind = UNITS[u][0]
            n = sum(1 for x in UNITS[:u + 1] if x[0] == kind)
            return {"k": k_done, "v": v_done, "hs": hs_done}[kind], n

        @block.sync
        def _(sp):
            sp.dma_start(condp, cond_pack[:]).then_inc(ld_cond, 16)
            sp.dma_start(projp[:], proj_pack[:]).then_inc(ld_proj, 16)
            sp.dma_start(xT[:], x_t[:]).then_inc(ld_x, 16)
            sp.dma_start(const[:], const_pack[:]).then_inc(ld_const, 16)
            sp.dma_start(selp[:], sel_pack[:]).then_inc(ld_const, 16)
            for k in range(2 * E):
                if k >= 2:
                    sp.wait_ge(w_done, k - 1)
                layer, e = divmod(k, E)
                w = (w_layer0, w_layer1)[layer]
                width = 2 * CHUNKS[layer] * 128
                sp.dma_start(raw[:, k % 2, 0:width], w[:, e, :]).then_inc(ld_w[k % 2], 16)
            for half in range(HALVES):
                sp.wait_ge(x1_done, HALVES + half + 1)
                sp.dma_start(out[:, half * HALF:(half + 1) * HALF],
                             x1[:, half * HALF:(half + 1) * HALF]).then_inc(stored, 16)
            sp.wait_ge(stored, 16 * HALVES)

        @block.tensor
        def _(pe):
            def mm(dst, lhs, rhs, start=True, stop=True, **kw):
                return nc.tensor.matmul(dst, lhs, rhs, start=start, stop=stop, **kw)

            def keep_warm(n, free_bank):
                for _ in range(n):
                    mm(free_bank[:], zeros[:, 0:128], zeros[:])

            pe.wait_ge(zeros_made, 1)
            keep_warm(WARM_UP, bank[7])
            pe.wait_ge(ld_cond, 16)
            a = COND_AT["wdec"][0]
            for n in range(2):
                for c in range(4):
                    m = mm(bank[1 + n][32 * c:32 * c + 32, :], CP("cond"),
                           condp[:, a + D * (8 * c + 4 * n):a + D * (8 * c + 4 * n + 4)], tile_position=(0, 32 * c))
                m.then_inc(u_mm, 1)
            cond = CP("cond")[:, 0:BATCH]
            mm(bank[0][:, 0:8], CP("ubias"), cond)
            mm(bank[0][:, 8:16], CP("kaff"), cond)
            mm(bank[0][:, 16:24], CP("oaff"), cond).then_inc(style_mm, 1)
            pe.wait_ge(ld_proj, 16)
            mm(bank[3][:, 0:QKV], PP("vt"), PP("w")).then_inc(wstack_mm, 1)
            pe.wait_ge(u_rows, 2)
            for k in range(8):
                nc.tensor.transpose(bank[4 + k // 4][:, 128 * (k % 4):128 * (k % 4 + 1)],
                                    urows[:, 128 * k:128 * (k + 1)], PP("ident")).then_inc(u_tr, 1)
            pe.wait_ge(u_done, 1)
            pe.wait_ge(u_copied, 1)
            pe.wait_ge(ld_x, 16)
            for b in range(BATCH):
                m = mm(bank[1 + b // PER_HALF][:, SEQ * (b % PER_HALF):SEQ * (b % PER_HALF + 1)],
                       urep[:, b, :, :].rearrange("p a b -> p (a b)"), xT[:, SEQ * b:SEQ * (b + 1)])
                if b % PER_HALF == PER_HALF - 1:
                    m.then_inc(t_mm, 1)
            pe.wait_ge(wstack_done, 1)
            for u, (kind, half, i) in enumerate(UNITS):
                if u == 0 or UNITS[u - 1][1] != half:
                    pe.wait_ge(t_done, half + 1)
                if u >= len(PROJ_BANKS):
                    pe.wait_ge(*unit_free(u - len(PROJ_BANKS)))
                dst = bank[PROJ_BANKS[u % len(PROJ_BANKS)]]
                tokens = slice(half * HALF, (half + 1) * HALF)
                if kind == "k":
                    m = mm(dst[:], wst[:, 1, 128 * i:128 * (i + 1)], ts[:, tokens])
                elif kind == "v":
                    for b in range(BATCH):
                        m = mm(dst[:, 64 * b:64 * (b + 1)], ts[:, SEQ * b:SEQ * (b + 1)], wc[:, 128:192])
                else:
                    m = mm(dst[:], vst[:], ts[:, tokens])
                m.then_inc(proj_mm, 1)

            pe.wait_ge(wsq_done, 2)
            pe.wait_ge(style_done, 1)
            for w in range(2):
                m = mm(bank[0][:, 32 + 8 * w:40 + 8 * w], wsq[:, w, :], style2[:, w, :])
            m.then_inc(demod_mm, 1)

            def queries(b):
                if b >= 2:
                    pe.wait_ge(q_done, b - 1)
                for G in range(GROUPS):
                    m = mm(bank[1 + b % 2][:, 128 * G:128 * (G + 1)], wst[:, 0, 128 * G:128 * (G + 1)],
                           ts[:, SEQ * b:SEQ * (b + 1)], start=G == 0, stop=False, skip_group_check=True)
                m.then_inc(q_mm, 1)

            def first_scores(b, r):
                if b >= 1:
                    pe.wait_ge(exp_done, 4 * (b - 1) + r + 1)
                rows = slice(32 * r, 32 * r + 8)
                for G in range(GROUPS):
                    m = mm(bank[3 + r][:, 128 * G:128 * (G + 1)], hi16[rows, b % 2, 128 * G:128 * (G + 1)],
                           kop[rows, G, SEQ * b:SEQ * (b + 1)], tile_position=(32 * r, 0))
                m.then_inc(s1_mm, 1)

            def minus_max(b):
                pe.wait_ge(mx_done, 4 * (b + 1))
                for G in range(GROUPS):
                    m = mm(bank[1 + b % 2][:, 128 * G:128 * (G + 1)], negm[:, b % 2, G, :], ident16[:],
                           start=False, stop=G == GROUPS - 1, skip_group_check=True)
                m.then_inc(negm_mm, 1)

            def sums(b, G):
                cols = slice(128 * G, 128 * (G + 1))
                for r in range(4):
                    h = 4 * G + r
                    m = mm(bank[7][32 * r:32 * r + 32, 0:SEQ], val[:, b, 32 * h:32 * h + 32],
                           probs[:, b % 2, r, cols], tile_position=(0, 32 * r),
                           start=G == 0, stop=G == GROUPS - 1, skip_group_check=True)
                if G == GROUPS - 1:
                    m.then_inc(av_mm, 1)

            def spread_sums(b):
                pe.wait_ge(av_read, b + 1)
                if b >= 1:
                    pe.wait_ge(ao_done, b)
                mm(bank[0][:, 0:SEQ], PP("spread"), av[:, b % 2, :]).then_inc(sums_mm, 1)

            def output_projection(b):
                pe.wait_ge(ao_done, b + 1)
                pe.wait_ge(ld_const, 32)
                mm(bank[7][:, 0:SEQ], C("ow"), ao[:, SEQ * b:SEQ * (b + 1)]).then_inc(mo_mm, 1)

            def logits(layer, t):
                pe.wait_ge(mo_done, layer * BATCH + t + 1)
                m = mm(bank[LOGIT_BANK[layer]][:, E * t:E * (t + 1)], mo[:, SEQ * t:SEQ * (t + 1)], C(f"rw{layer}"))
                if t == BATCH - 1:
                    m.then_inc(rt_mm, 1)

            queries(0)
            for u in range(len(UNITS) - len(PROJ_BANKS), len(UNITS)):
                pe.wait_ge(*unit_free(u))
            pe.wait_ge(q_hi, 1)
            for r in range(4):
                first_scores(0, r)
            minus_max(0)
            for b in range(BATCH):
                if b + 1 < BATCH:
                    queries(b + 1)
                pe.wait_ge(q_done, b + 1)
                for r in range(4):
                    rows = slice(32 * r, 32 * r + 32)
                    for G in range(GROUPS):
                        m = mm(bank[3 + r][:, 128 * G:128 * (G + 1)], kop[rows, G, SEQ * b:SEQ * (b + 1)],
                               qop[rows, b % 2, 128 * G:128 * (G + 1)], tile_position=(32 * r, 0))
                    m.then_inc(s2_mm, 1)
                if b == 1:
                    pe.wait_ge(demod_done, 1)
                if b >= 1:
                    spread_sums(b - 1)
                if b >= 2:
                    output_projection(b - 2)
                if b + 1 < BATCH:
                    pe.wait_ge(q_hi, b + 2)
                    for r in range(4):
                        first_scores(b + 1, r)
                if b == 0:
                    pe.wait_ge(v_done, 1)
                if b >= 2:
                    pe.wait_ge(mo_done, b - 1)
                pe.wait_ge(exp_done, 4 * (b + 1))
                for G in range(GROUPS):
                    sums(b, G)
                    if b + 1 < BATCH and G == MAX_AFTER:
                        minus_max(b + 1)
            for t in range(BATCH - 2):
                logits(0, t)
            spread_sums(BATCH - 1)
            output_projection(BATCH - 2)
            logits(0, BATCH - 2)
            keep_warm(4, bank[3])
            output_projection(BATCH - 1)
            keep_warm(2, bank[3])
            logits(0, BATCH - 1)

            def route(layer):
                pe.wait_ge(parts_done, layer + 1)
                for half in range(HALVES):
                    for t in range(PER_HALF):
                        m = nc.tensor.transpose(bank[(0, 6)[half]][0:16, 128 * t:128 * (t + 1)],
                                                parts[:, half * PER_HALF + t, :].bitcast(F32), C("ident"))
                    m.then_inc(parts_tr, 1)

            def broadcast(j):
                _, e, half = JOBS[j]
                if j >= 2:
                    pe.wait_ge(cb_read, j - 1)
                mm(bank[5 + j % 2][:], sel[:, 128 * e:128 * (e + 1)], comb_t[:, half, :]).then_inc(cb_mm, 1)

            def modulated_keys(half):
                if half == 0:
                    pe.wait_ge(diag_done, 1)
                else:
                    pe.wait_ge(wmod_done, half)
                for b in range(half * PER_HALF, (half + 1) * PER_HALF):
                    m = mm(bank[0][:, SEQ * (b % PER_HALF):SEQ * (b % PER_HALF + 1)], C("wk"), diag[:, b, :])
                m.then_inc(wmod_mm, 1)

            def slots(k, first, count):
                base = weight_slot(k) + 128 * first
                return slice(base, base + 128 * count)

            def first_product(c):
                j, fc = CHUNK_LIST[c]
                layer, e, half = JOBS[j]
                k = layer * E + e
                if fc == 0:
                    if e == 0:
                        pe.wait_ge(mo_split, layer * HALVES + half + 1)
                    pe.wait_ge(w_done, k + 1)
                if c >= 3:
                    pe.wait_ge(lo_done, c - 2)
                tokens = slice(half * HALF, (half + 1) * HALF)
                at = slots(k, fc, 1)
                dst = bank[1 + c % 3][:]
                mm(dst, w_hi[:, at], mo_hi[:, tokens], stop=False)
                mm(dst, w_hi[:, at], mo_lo[:, tokens], start=False, stop=False)
                mm(dst, w_lo[:, at], mo_hi[:, tokens], start=False).then_inc(h_mm, 1)

            def second_product(c):
                j, fc = CHUNK_LIST[c]
                layer, e, half = JOBS[j]
                k = layer * E + e
                n = CHUNKS[layer]
                if fc == 0 and e > 0:
                    broadcast(j)
                if fc == 0 and j >= 2:
                    pe.wait_ge(weighted_done, j - 1)
                pe.wait_ge(lo_done, c + 1)
                at = slots(k, n + fc, 1)
                dst = bank[(4, 7)[j % 2]][:]
                mm(dst, w_hi[:, at], g_hi[:, c % 3, :], start=fc == 0, stop=False)
                mm(dst, w_hi[:, at], g_lo[:, c % 3, :], start=False, stop=False)
                mm(dst, w_lo[:, at], g_hi[:, c % 3, :], start=False, stop=fc == n - 1).then_inc(y_mm, 1)

            def experts(layer):
                first, end = FIRST_CHUNK[layer * JOBS_PER_LAYER], END_CHUNK[(layer + 1) * JOBS_PER_LAYER - 1]
                for c in range(first, end + LAG):
                    if c < end:
                        first_product(c)
                    if c == first + ROUTE_AFTER[layer] + 1:
                        pe.wait_ge(sel_done, 1)
                        pe.wait_ge(comb_done, HALVES * (layer + 1))
                        broadcast(layer * JOBS_PER_LAYER)
                        broadcast(layer * JOBS_PER_LAYER + 1)
                    if c == first + LAG:
                        keep_warm(START_FILL[layer], bank[5])
                    if c - LAG >= first:
                        second_product(c - LAG)
                    if c == first + ROUTE_AFTER[layer]:
                        route(layer)
                    if layer == 0 and c in WMOD_AFTER:
                        modulated_keys(WMOD_AFTER.index(c))

            experts(0)

            for half in range(HALVES):
                pe.wait_ge(x1_done, half + 1)
                if half == 0:
                    pe.wait_ge(wmod_done, HALVES)
                for b in range(half * PER_HALF, (half + 1) * PER_HALF):
                    m = mm(bank[1 + half][:, SEQ * (b % PER_HALF):SEQ * (b % PER_HALF + 1)],
                           x1[:, SEQ * b:SEQ * (b + 1)], wmod[:, b, :])
                m.then_inc(kx_mm, 1)

            def output(b):
                pe.wait_ge(att_read, b + 1)
                if b >= 2:
                    pe.wait_ge(mo_done, BATCH + b - 1)
                mm(bank[5 + b % 2][:, 0:SEQ], C("wo_t"), att_t[:, b % 2, :]).then_inc(mo_mm, 1)

            for b in range(BATCH):
                if b >= 2:
                    pe.wait_ge(att_read, b - 1)
                pe.wait_ge(far_sum, b + 1)
                near = NEAR_SLOTS if b < FOLDED else NEAR_SLOTS[:5]
                for s in FAR_LEFT + near:
                    if s == near[0]:
                        pe.wait_ge(*((prod_near, b + 1) if b < FOLDED else (near_sum, b - FOLDED + 1)))
                    m = mm(bank[3 + b % 2][:, 0:128], prod[:, b % 2, 128 * s:128 * (s + 1)], C("ident"),
                           start=s == FAR_LEFT[0], stop=s == near[-1])
                m.then_inc(att_mm, 1)
                if b >= 1:
                    output(b - 1)
                if b >= 2:
                    logits(1, b - 2)
            output(BATCH - 1)
            logits(1, BATCH - 2)
            logits(1, BATCH - 1)
            experts(1)

        @block.scalar
        def _(act):
            def activate(dst, src, func, **kw):
                return nc.scalar.activation(dst, src, func, **kw)

            nc.scalar.preload_act_table_set("natural_log_exp_and_others")
            act.wait_ge(u_mm, 2)
            activate(urows[:, 512:1024], bank[2][:], ACT.Copy).then_inc(u_rows, 1)
            act.wait_ge(u_tr, 8)
            for blk in range(4):
                ins = activate(*u_copy(blk, 1), ACT.Copy)
            ins.then_inc(u_copied, 1)
            act.wait_ge(ubias_done, 1)
            for b in range(BATCH):
                if b % PER_HALF == 0:
                    act.wait_ge(t_mm, b // PER_HALF + 1)
                activate(ts[:, SEQ * b:SEQ * (b + 1)],
                         bank[1 + b // PER_HALF][:, SEQ * (b % PER_HALF):SEQ * (b % PER_HALF + 1)],
                         ACT.Identity, bias=ubias[:, b:b + 1]).then_inc(t_hi, 1)
            nk = 0
            for u, (kind, half, i) in enumerate(UNITS):
                src = bank[PROJ_BANKS[u % len(PROJ_BANKS)]][:]
                if kind == "hs":
                    continue
                act.wait_ge(proj_mm, u + 1)
                if kind == "k":
                    if nk >= 2:
                        act.wait_ge(k_done, nk - 1)
                    activate(hi16[:, nk % 2, :], src, ACT.Copy).then_inc(k_hi, 1)
                    nk += 1
                else:
                    act.wait_ge(val_clear, 1)
                    for G in range(GROUPS):
                        ins = activate(view(val[:], (128 + KPH) * G, [[512, BATCH], [32, 4], [1, KPH]]),
                                       view(src, 4 * KPH * G, [[HEADS * KPH, BATCH], [KPH, 4], [1, KPH]]), ACT.Copy)
                    ins.then_inc(v_done, 1)

            def query_parts(b):
                act.wait_ge(q_mm, b + 1)
                if b < 2:
                    act.wait_ge(k_done, GROUPS * HALVES)
                else:
                    act.wait_ge(q_done, b - 1)
                activate(hi16[:, b % 2, :], bank[1 + b % 2][:], ACT.Copy).then_inc(q_hi, 1)

            def first_output(b):
                act.wait_ge(mo_mm, b + 1)
                activate(mo[:, SEQ * b:SEQ * (b + 1)], bank[7][:, 0:SEQ], ACT.Identity, bias=C("ob0")).then_inc(mo_done, 1)

            def read_values(b):
                act.wait_ge(av_mm, b + 1)
                if b >= 2:
                    act.wait_ge(ao_done, b - 1)
                activate(av[:, b % 2, :], bank[7][:, 0:SEQ], ACT.Copy).then_inc(av_read, 1)

            def inverse_sums(b):
                act.wait_ge(sums_mm, b + 1)
                if b >= 1:
                    act.wait_ge(ao_done, b)
                activate(rz[:], bank[0][:, 0:SEQ], ACT.Ln).then_inc(log_done, 1)
                act.wait_ge(log_done, b + 1)
                activate(rz[:], rz[:], ACT.Exp, scale=-1.0).then_inc(inv_done, 1)

            query_parts(0)
            act.wait_ge(demod_mm, 1)
            flat = demod[:].rearrange("p w b -> p (w b)")
            activate(flat, bank[0][:, 32:48], ACT.Ln, bias=eps[:]).then_inc(demod_log, 1)
            act.wait_ge(demod_log, 1)
            activate(flat, flat, ACT.Exp, scale=-0.5).then_inc(demod_read, 1)
            for b in range(BATCH):
                if b + 1 < BATCH:
                    query_parts(b + 1)
                if b >= 1:
                    read_values(b - 1)
                for r in range(4):
                    act.wait_ge(s2_mm, 4 * b + r + 1)
                    if b >= 2 and r == 0:
                        act.wait_ge(av_mm, b - 1)
                    activate(probs[:, b % 2, r, :], bank[3 + r][:], ACT.Exp,
                             scale=float(KPH) ** -0.5).then_inc(exp_done, 1)
                if b >= 2:
                    first_output(b - 2)
                if b >= 1:
                    inverse_sums(b - 1)
            read_values(BATCH - 1)
            inverse_sums(BATCH - 1)
            first_output(BATCH - 2)

            def soft(q):
                act.wait_ge(sub_done, q + 1)
                pair = amat[:, q % 2, :, :, :].rearrange("p t s h -> p (t s h)")
                activate(pair, pair, ACT.Exp, scale=float(D1) ** -0.5).then_inc(soft_exp, 1)

            def block_output(b):
                act.wait_ge(mo_mm, BATCH + b + 1)
                activate(mo[:, SEQ * b:SEQ * (b + 1)], bank[5 + b % 2][:, 0:SEQ],
                         ACT.Identity, scale=demod[:, 1, b:b + 1], bias=C("ob1")).then_inc(mo_done, 1)

            def routing(layer):
                act.wait_ge(rt_sub, layer + 1)
                activate(rt[:, 1, :, :], rt[:, 0, :, :], ACT.Exp).then_inc(rt_exp, 1)

            def experts(layer):
                for c in range(FIRST_CHUNK[layer * JOBS_PER_LAYER], END_CHUNK[(layer + 1) * JOBS_PER_LAYER - 1]):
                    j, fc = CHUNK_LIST[c]
                    _, e, half = JOBS[j]
                    act.wait_ge(h_mm, c + 1)
                    if c >= 3:
                        act.wait_ge(y_mm, c - 2)
                    a = CONST_AT["b1"][0] + CHUNKS[0] * e + fc
                    bias = dict(bias=const[:, a:a + 1]) if layer == 0 else {}
                    h = bank[1 + c % 3][:]
                    activate(g_hi[:, c % 3, :], h, ACT.Gelu, **bias)
                    activate(h, h, ACT.Gelu, **bias).then_inc(gelu_done, 1)
                    if layer == 0 and c in WMOD_AFTER:
                        half = WMOD_AFTER.index(c)
                        act.wait_ge(wmod_mm, half + 1)
                        for b in range(half * PER_HALF, (half + 1) * PER_HALF):
                            ins = activate(wmod[:, b, :], bank[0][:, SEQ * (b % PER_HALF):SEQ * (b % PER_HALF + 1)],
                                           ACT.Copy, scale=style[:, 0, b:b + 1])
                        ins.then_inc(wmod_done, 1)

            first_output(BATCH - 1)
            routing(0)
            experts(0)

            for half in range(HALVES):
                act.wait_ge(kx_done, half + 1)
                rows = kx2[:, half * PER_HALF:(half + 1) * PER_HALF, :]
                activate(rows[:, :, 128:256], rows[:, :, 0:128], ACT.Copy).then_inc(kx_dup, 1)
                if half == 0:
                    soft(0)
            for b in range(BATCH):
                if b % 2 == 0 and b + 2 < BATCH:
                    soft(b // 2 + 1)
                act.wait_ge(att_mm, b + 1)
                if b >= 2:
                    act.wait_ge(mo_mm, BATCH + b - 1)
                activate(att_t[:, b % 2, :], bank[3 + b % 2][:, 0:128], ACT.Copy,
                         scale=style[:, 1, b:b + 1]).then_inc(att_read, 1)
                if b >= 1:
                    block_output(b - 1)
            block_output(BATCH - 1)
            routing(1)
            experts(1)

        @block.vector
        def _(dve):
            v = nc.vector
            linked = [0]

            def link(ins):
                ins.then_inc(dve_chain, 1)
                linked[0] += 1
                dve.wait_ge(dve_chain, linked[0])

            v.memset(zeros[:], 0.0).then_inc(zeros_made, 1)
            v.memset(negm[:], 0.0)
            v.memset(eps[:], DEMOD_EPS)
            link(v.memset(wst[:].bitcast(F32), 0.0))
            dve.wait_ge(u_mm, 1)
            v.tensor_copy(urows[:, 0:512], bank[1][:]).then_inc(u_rows, 1)
            dve.wait_ge(ld_proj, 16)
            dve.wait_ge(wstack_mm, 1)
            link(v.tensor_tensor(wfull[:], bank[3][:, 0:QKV], PP("bias"), ALU.add))
            v.tensor_copy(ident16[:], PP("ident"))
            dve.wait_ge(u_tr, 8)
            for blk in range(4):
                ins = v.tensor_copy(*u_copy(blk, 0))
            ins.then_inc(u_done, 1)
            dve.wait_ge(style_mm, 1)
            v.tensor_copy(ubias[:], bank[0][:, 0:8]).then_inc(ubias_done, 1)
            link(v.tensor_copy(style[:].rearrange("p w b -> p (w b)"), bank[0][:, 8:24]))
            v.tensor_tensor(style2[:], style[:], style[:], ALU.mult).then_inc(style_done, 1)
            v.tensor_copy(wc[:], wfull[:])
            link(v.tensor_copy(vst[:], PP("vrep")))
            for rows in (slice(32, 64), slice(96, 128)):
                v.tensor_tensor(vst[rows, :], PP("vrep")[rows, :], vst[rows, :].bitcast(F32), ALU.subtract)
                ins = v.tensor_tensor(wc[rows, :], wfull[rows, :], wc[rows, :].bitcast(F32), ALU.subtract)
            link(ins)
            for w in range(2):
                v.tensor_copy(view(wst[:, w, :], 0, [[32, HEADS], [4, 4], [1, KPH]]),
                              view(wc[:], 64 * w, [[KPH, HEADS], [0, 4], [1, KPH]]).bitcast(F32))
            v.tensor_copy(view(wst[:, 1, :], 16, [[32, HEADS]]), PP("one").to_broadcast([128, HEADS])).then_inc(wstack_done, 1)
            for b in range(BATCH):
                dve.wait_ge(t_hi, PER_HALF * (b // PER_HALF + 1))
                cols = slice(SEQ * b, SEQ * (b + 1))
                ins = v.scalar_tensor_tensor(
                    ts[64:128, cols], bank[1 + b // PER_HALF][64:128, SEQ * (b % PER_HALF):SEQ * (b % PER_HALF + 1)],
                    ubias[64:128, b:b + 1], ts[64:128, cols].bitcast(F32), ALU.add, ALU.subtract)
                if b % PER_HALF == PER_HALF - 1:
                    ins.then_inc(t_done, 1)
            nk = 0
            for u, (kind, half, i) in enumerate(UNITS):
                src = bank[PROJ_BANKS[u % len(PROJ_BANKS)]][:]
                tokens = slice(half * HALF, (half + 1) * HALF)
                if kind == "k":
                    nk += 1
                    dve.wait_ge(k_hi, nk)
                    v.scalar_tensor_tensor(kop[:, i, tokens], hi16[:, (nk - 1) % 2, :], PP("mk"), src,
                                           ALU.mult, ALU.add).then_inc(k_done, 1)
                elif kind == "hs":
                    dve.wait_ge(proj_mm, u + 1)
                    v.tensor_tensor(xhs[:, tokens], src, xT[:, tokens], ALU.add).then_inc(hs_done, 1)
            def normalise(b):
                dve.wait_ge(inv_done, b + 1)
                link(v.tensor_tensor(newton[:], bank[0][:, 0:SEQ], rz[:], ALU.mult))
                link(v.scalar_tensor_tensor(newton[:], newton[:], 2.0, rz[:], ALU.subtract, ALU.mult))
                v.scalar_tensor_tensor(ao[:, SEQ * b:SEQ * (b + 1)], av[:, b % 2, :], -1.0, newton[:],
                                       ALU.mult, ALU.mult).then_inc(ao_done, 1)

            def split_output(layer, half):
                tokens = slice(half * HALF, (half + 1) * HALF)
                dve.wait_ge(mo_done, layer * BATCH + PER_HALF * (half + 1))
                link(v.tensor_copy(mo_hi[:, tokens], mo[:, tokens]))
                v.tensor_tensor(mo_lo[:, tokens], mo[:, tokens], mo_hi[:, tokens].bitcast(F32),
                                ALU.subtract).then_inc(mo_split, 1)

            def demodulation():
                flat = demod[:].rearrange("p w b -> p (w b)")
                dve.wait_ge(demod_read, 1)
                link(v.tensor_tensor(demod_step[:], flat, flat, ALU.mult))
                link(v.scalar_tensor_tensor(demod_step[:], bank[0][:, 32:48], DEMOD_EPS, demod_step[:], ALU.add, ALU.mult))
                link(v.tensor_scalar(demod_step[:], demod_step[:], -0.5, 1.5, ALU.mult, ALU.add))
                v.tensor_tensor(flat, flat, demod_step[:], ALU.mult).then_inc(demod_done, 1)
                dve.wait_ge(demod_done, 1)
                for b in range(BATCH):
                    ins = v.tensor_scalar(diag[:, b, :], PP("ident"), demod[:, 0, b:b + 1], None, ALU.mult)
                ins.then_inc(diag_done, 1)

            for b in range(BATCH):
                for r in range(4):
                    dve.wait_ge(s1_mm, 4 * b + r + 1)
                    if b >= 2 and r == 0:
                        dve.wait_ge(negm_mm, b - 1)
                    v.tensor_reduce(negm[:, b % 2, :, 32 * r + 16:32 * r + 17],
                                    bank[3 + r][:].rearrange("p (g t) -> p g t", g=GROUPS),
                                    AX.X, ALU.max, negate=True).then_inc(mx_done, 1)
                dve.wait_ge(negm_mm, b + 1)
                dve.wait_ge(q_hi, b + 1)
                v.scalar_tensor_tensor(qop[:, b % 2, :], hi16[:, b % 2, :], PP("mq"), bank[1 + b % 2][:],
                                       ALU.mult, ALU.add).then_inc(q_done, 1)
                if b == 0:
                    demodulation()
                if b == BATCH - 2:
                    split_output(0, 0)
                if b >= 2:
                    normalise(b - 2)
            dve.wait_ge(ld_const, 32)
            v.tensor_copy(sel[:], selp[:]).then_inc(sel_done, 1)
            normalise(BATCH - 2)
            normalise(BATCH - 1)

            def routing(layer):
                wide = [128, BATCH, E]
                logits, p, one, key, two, rest = (rt[:, i, :, :] for i in (2, 1, 3, 4, 5, 6))
                top, inv, most, second, total = (rs[:, i, :, :] for i in (0, 1, 2, 3, 4))
                src = bank[LOGIT_BANK[layer]][:, 0:BATCH * E].rearrange("p (t e) -> p t e", t=BATCH)
                rank = C("rank").rearrange("p (t e) -> p t e", t=BATCH)

                def pick(dst, values, largest):
                    link(v.tensor_tensor(key, values, largest.to_broadcast(wide), ALU.is_equal))
                    link(v.tensor_tensor(key, key, rank, ALU.mult))
                    link(v.tensor_reduce(most, key, AX.X, ALU.max))
                    link(v.tensor_tensor(dst, key, most.to_broadcast(wide), ALU.is_equal))

                dve.wait_ge(rt_mm, layer + 1)
                if layer == 0:
                    link(v.tensor_tensor(logits, src, C("rb").rearrange("p (t e) -> p t e", t=BATCH), ALU.add))
                else:
                    link(v.tensor_copy(logits, src))
                link(v.tensor_reduce(top, logits, AX.X, ALU.max))
                v.tensor_tensor(rt[:, 0, :, :], logits, top.to_broadcast(wide), ALU.subtract).then_inc(rt_sub, 1)
                split_output(layer, 1)
                dve.wait_ge(rt_exp, layer + 1)
                first = FIRST_CHUNK[layer * JOBS_PER_LAYER]
                v.tensor_reduce(total, p, AX.X, ALU.add)
                link(v.tensor_reduce(top, p, AX.X, ALU.max))
                pick(one, p, top)
                lower_part(first)
                link(v.scalar_tensor_tensor(rest, one, -2.0, p, ALU.mult, ALU.add))
                link(v.tensor_reduce(second, rest, AX.X, ALU.max))
                lower_part(first + 1)
                pick(two, rest, second)
                lower_part(first + 2)
                link(v.tensor_tensor(one, one, two, ALU.add))
                v.tensor_tensor(one, one, p, ALU.mult)
                link(v.tensor_tensor(inv, top, second, ALU.add))
                if layer == 0:
                    link(v.scalar_tensor_tensor(inv, total, TOP_EPS, inv, ALU.mult, ALU.add))
                link(v.reciprocal(inv, inv))
                lower_part(first + 3)
                link(v.tensor_tensor(one, one, inv.to_broadcast(wide), ALU.mult))
                link(v.tensor_copy(parts[:, :, 0:E], one))
                v.tensor_tensor(parts[:, :, E:2 * E], one, parts[:, :, 0:E].bitcast(F32),
                                ALU.subtract).then_inc(parts_done, 1)
                for c in range(first + 4, first + ROUTE_AFTER[layer]):
                    lower_part(c)
                for half in range(HALVES):
                    dve.wait_ge(parts_tr, layer * HALVES + half + 1)
                    v.tensor_copy(comb_t[:, half, :], bank[(0, 6)[half]][0:16, :]).then_inc(comb_done, 1)
                broadcast_read(layer * JOBS_PER_LAYER)
                weigh(layer * JOBS_PER_LAYER)
                broadcast_read(layer * JOBS_PER_LAYER + 1)

            def weigh(j):
                dve.wait_ge(y_mm, END_CHUNK[j])
                dve.wait_ge(cb_read, j + 1)
                if j >= 2 and by_gpsimd(j - 2):
                    dve.wait_ge(acc_done, accumulated(j - 2))
                layer, e, half = JOBS[j]
                y = bank[(4, 7)[j % 2]][:]
                if layer == 0:
                    ins = v.scalar_tensor_tensor(weighted[:, j % 2, :], y, C("b2")[:, e:e + 1], cbs[:, j % 2, :],
                                                 ALU.add, ALU.mult)
                else:
                    ins = v.tensor_tensor(weighted[:, j % 2, :], y, cbs[:, j % 2, :], ALU.mult)
                ins.then_inc(weighted_done, 1)
                if not by_gpsimd(j):
                    tokens = slice(half * HALF, (half + 1) * HALF)
                    dve.wait_ge(weighted_done, j + 1)
                    dve.wait_ge(acc_done, accumulated(j - HALVES))
                    v.tensor_tensor(x1[:, tokens], x1[:, tokens], weighted[:, j % 2, :], ALU.add).then_inc(x1_done, 1)

            def lower_part(c):
                dve.wait_ge(gelu_done, c + 1)
                if c >= 3:
                    dve.wait_ge(y_mm, c - 2)
                v.tensor_tensor(g_lo[:, c % 3, :], bank[1 + c % 3][:], g_hi[:, c % 3, :].bitcast(F32),
                                ALU.subtract).then_inc(lo_done, 1)

            def broadcast_read(j):
                dve.wait_ge(cb_mm, j + 1)
                if j >= 2:
                    dve.wait_ge(weighted_done, j - 1)
                scale = (MOE_SCALE, 1.0)[JOBS[j][0]]
                v.tensor_scalar(cbs[:, j % 2, :], bank[5 + j % 2][:], scale, None, ALU.mult).then_inc(cb_read, 1)

            def experts(layer):
                first_job = layer * JOBS_PER_LAYER
                first, end = FIRST_CHUNK[first_job], END_CHUNK[first_job + JOBS_PER_LAYER - 1]
                for c in range(first + ROUTE_AFTER[layer], end + LAG):
                    if c < end:
                        lower_part(c)
                    j, fc = CHUNK_LIST[c - LAG]
                    if fc == 0 and j >= first_job + HALVES:
                        broadcast_read(j)
                    if END_CHUNK[j] == c - LAG + 1 and j > first_job:
                        weigh(j)

            routing(0)
            experts(0)
            def keys(half):
                dve.wait_ge(kx_mm, half + 1)
                v.tensor_tensor(kx2[:, half * PER_HALF:(half + 1) * PER_HALF, 0:128],
                                bank[1 + half][:].rearrange("p (t c) -> p t c", t=PER_HALF),
                                view(C("kb"), 0, [[0, PER_HALF], [1, 128]]), ALU.add).then_inc(kx_done, 1)

            def mark(ins):
                ins.then_inc(dve_chain, 1)
                linked[0] += 1
                return linked[0]

            def head_products(q):
                pair = kx2[:, 2 * q:2 * q + 2, :]
                dve.wait_ge(kx_dup, q // 2 + 1)
                return mark(v.tensor_tensor(dots.rearrange("p (t s c) -> p t s c", t=2, s=NEAR),
                                            view(pair, 0, [[256, 2], [0, NEAR], [1, 128]]),
                                            view(pair, 0, [[256, 2], [D1, NEAR], [1, 128]]), ALU.mult))

            def near_scores(q, done):
                dve.wait_ge(dve_chain, done)
                return mark(v.tensor_reduce(gram[:, :, 0:NEAR, 0:H1],
                                            dots.rearrange("p (t s h d) -> p t s h d", t=2, s=NEAR, h=H1), AX.X, ALU.add))

            def double_heads(q, done):
                dve.wait_ge(dve_chain, done)
                return mark(v.tensor_copy(gram[:, :, 1:H1 // 2, H1:2 * H1], gram[:, :, 1:H1 // 2, 0:H1]))

            def far_scores(q, done):
                dve.wait_ge(dve_chain, done)
                return mark(v.tensor_copy(gram[:, :, NEAR:H1, 0:H1],
                                          view(gram[:], 2 * H1 + H1 - 1, [[2 * H1 * H1, 2], [2 * H1 - 1, H1 // 2 - 1], [1, H1]])))

            def maxima(q, done):
                dve.wait_ge(dve_chain, done)
                return mark(v.tensor_reduce(small[:, q % 2, 0, :, :], gram[:, :, :, 0:H1].rearrange("p t s h -> p t h s"),
                                            AX.X, ALU.max))

            def less_maximum(q, done):
                dve.wait_ge(dve_chain, done)
                if q >= 2:
                    dve.wait_ge(prod_far, 2 * q - 2)
                v.tensor_tensor(amat[:, q % 2, :, :, :], gram[:, :, :, 0:H1],
                                view(small[:, q % 2, 0, :, :], 0, [[H1, 2], [0, H1], [1, H1]]),
                                ALU.subtract).then_inc(sub_done, 1)

            def exponentials_sum(q):
                dve.wait_ge(soft_exp, q + 1)
                return mark(v.tensor_reduce(small[:, q % 2, 1, :, :], amat[:, q % 2, :, :, :].rearrange("p t s h -> p t h s"),
                                            AX.X, ALU.add))

            def inverse(q, done):
                dve.wait_ge(dve_chain, done)
                return mark(v.reciprocal(small[:, q % 2, 1, :, :], small[:, q % 2, 1, :, :]))

            def weights(q, done):
                dve.wait_ge(dve_chain, done)
                v.tensor_tensor(amat[:, q % 2, :, :, :], amat[:, q % 2, :, :, :],
                                view(small[:, q % 2, 1, :, :], 0, [[H1, 2], [0, H1], [1, H1]]), ALU.mult).then_inc(a_done, 1)

            def near_values(b):
                dve.wait_ge(a_done, b // 2 + 1)
                if b >= 2:
                    dve.wait_ge(att_mm, b - 1)
                v.tensor_tensor(prod[:, b % 2, 0:NEAR * 128].rearrange("p (s h d) -> p s h d", s=NEAR, h=H1),
                                view(amat[:, b // 2 % 2, b % 2, :, :], 0, [[H1, NEAR], [1, H1], [0, D1]]),
                                view(kx2[:, b, :], 0, [[D1, NEAR], [D1, H1], [1, D1]]), ALU.mult).then_inc(prod_near, 1)

            def fold(b):
                if b >= FOLDED:
                    dve.wait_ge(prod_near, b + 1)
                    first, second = (prod[:, b % 2, 128 * n:128 * (n + 4)] for n in (1, 5))
                    v.tensor_tensor(first, first, second, ALU.add).then_inc(near_sum, 1)

            keys(0)
            s = head_products(0)
            s = near_scores(0, s)
            s = double_heads(0, s)
            s = far_scores(0, s)
            s = maxima(0, s)
            less_maximum(0, s)
            keys(1)
            for q in range(BATCH // 2 - 1):
                s = head_products(q + 1)
                w = exponentials_sum(q)
                s = near_scores(q + 1, s)
                w = inverse(q, w)
                s = double_heads(q + 1, s)
                weights(q, w)
                s = far_scores(q + 1, s)
                near_values(2 * q)
                s = maxima(q + 1, s)
                fold(2 * q)
                near_values(2 * q + 1)
                less_maximum(q + 1, s)
                fold(2 * q + 1)
            q = BATCH // 2 - 1
            w = exponentials_sum(q)
            w = inverse(q, w)
            weights(q, w)
            for b in (2 * q, 2 * q + 1):
                near_values(b)
                fold(b)
            split_output(1, 0)
            routing(1)
            experts(1)

        @block.gpsimd
        def _(pool):
            p = nc.gpsimd

            p.memset(val[:], 0.0).then_inc(val_zero, 1)
            pool.wait_ge(val_zero, 1)
            p.memset(view(val[:], 16, [[512, BATCH], [129, GROUPS], [32, 4]]), 1.0).then_inc(val_clear, 1)

            def split_weights(k):
                if k >= 2 * E:
                    return
                width = 2 * CHUNKS[k // E] * 128
                pool.wait_ge(ld_w[k % 2], 16 * (k // 2 + 1))
                if slot_free(k) is not None:
                    pool.wait_ge(y_mm, END_CHUNK[slot_free(k) * HALVES + HALVES - 1])
                at = slice(weight_slot(k), weight_slot(k) + width)
                p.tensor_copy(w_hi[:, at], raw[:, k % 2, 0:width]).then_inc(pool_chain, 1)
                pool.wait_ge(pool_chain, k + 1)
                p.tensor_tensor(w_lo[:, at], raw[:, k % 2, 0:width], w_hi[:, at].bitcast(F32),
                                ALU.subtract).then_inc(w_done, 1)

            def accumulate(j):
                layer, _, half = JOBS[j]
                tokens = slice(half * HALF, (half + 1) * HALF)
                pool.wait_ge(weighted_done, j + 1)
                before = xhs if j < HALVES else x1
                if j >= 1:
                    pool.wait_ge(acc_done, accumulated(j) - 1)
                p.tensor_tensor(x1[:, tokens], before[:, tokens], weighted[:, j % 2, :], ALU.add).then_inc(acc_done, 1)

            def layer_of_experts(layer):
                for e in range(E):
                    k = layer * E + e
                    if layer == 0 and e in (1, 2, 4):
                        split_weights({1: 6, 2: 7, 4: 8}[e])
                    elif layer == 1:
                        split_weights(k + 2)
                    for half in range(HALVES):
                        if by_gpsimd(k * HALVES + half):
                            accumulate(k * HALVES + half)

            for k in range(6):
                split_weights(k)
                if k == 0:
                    pool.wait_ge(ld_const, 32)
                    for w, name in enumerate(("wk_t", "wo_t")):
                        p.tensor_tensor(wsq[:, w, :], C(name), C(name), ALU.mult).then_inc(wsq_done, 1)
            layer_of_experts(0)
            split_weights(E + 1)
            for b in range(BATCH):
                i = b % 2
                pool.wait_ge(a_done, b // 2 + 1)
                if b >= 2:
                    pool.wait_ge(att_mm, b - 1)
                p.tensor_tensor(prod[:, i, NEAR * 128:].rearrange("p (s h d) -> p s h d", s=H1 - NEAR, h=H1),
                                view(amat[:, b // 2 % 2, b % 2, :, :], H1 * NEAR, [[H1, H1 - NEAR], [1, H1], [0, D1]]),
                                view(kx2[:, b, :], D1 * (H1 - 1), [[-D1, H1 - NEAR], [D1, H1], [1, D1]]),
                                ALU.mult).then_inc(prod_far, 1)
                pool.wait_ge(prod_far, b + 1)
                first, second = (prod[:, i, 128 * n:128 * (n + 3)] for n in (NEAR, NEAR + 3))
                p.tensor_tensor(first, first, second, ALU.add).then_inc(far_sum, 1)
            pool.wait_ge(kx_mm, HALVES)
            layer_of_experts(1)


def kernel(**inputs):
    import numpy as np
    import concourse.bacc as bacc
    from concourse.bass_utils import run_bass_kernel_spmd

    t = {k: np.asarray(v) for k, v in inputs.items()}
    f32 = np.float32

    cond = np.zeros((COND + 1, ROWS), f32)
    cond[:COND, :BATCH] = t["cond_512"].T
    cond[COND, :BATCH] = 1.0
    wdec = np.concatenate([t["L0_cond_W_dec"], t["L0_cond_b_dec"][None]], 0).reshape(COND + 1, D + 1, RANK)
    ubias = np.zeros((COND + 1, 4, 32), f32)
    ubias[:, :, :RANK] = wdec[:, D, None, :]
    ubias[COND, :, RANK] = 1.0
    kaff = np.concatenate([t["L1_cond_k_aff_w"].T, t["L1_cond_k_aff_b"][None]], 0)
    oaff = np.concatenate([t["L1_cond_o_aff_w"].T, t["L1_cond_o_aff_b"][None]], 0)
    by_rank = np.zeros((COND + 1, ROWS, D), f32)
    by_rank[:, :RANK] = wdec[:, :D].transpose(0, 2, 1)
    cond_pack = np.concatenate([cond, ubias.reshape(COND + 1, 128), kaff, oaff, by_rank.reshape(COND + 1, ROWS * D)], 1)

    V = t["L0_cond_V"]
    vrep = np.zeros((4, 32, D), f32)
    vrep[:, :RANK] = V[None]
    vrep = vrep.reshape(128, D)
    def first_columns(q):
        return q.reshape(-1, HEADS, 2 * KPH)[:, :, :KPH].reshape(-1, HEADS * KPH)

    w_qkv = np.concatenate([first_columns(t["L0_ffn_q_w"]), t["L0_ffn_k_w"], t["L0_ffn_v_w"]], 1)
    bias = np.zeros((4, 32, QKV), f32)
    bias[:, RANK] = np.concatenate([first_columns(t["L0_ffn_q_b"][None]), t["L0_ffn_k_b"][None], t["L0_ffn_v_b"][None]], 1)
    row = np.arange(128) % 32
    mq = np.where((row >= 8) & (row < 16), -1.0, 0.0).astype(f32)[:, None]
    mk = np.where((row < 16) & (row % 8 >= 4), -1.0, 0.0).astype(f32)[:, None]
    one = np.zeros((128, 1), f32)
    one[RANK] = 1.0
    spread = np.zeros((4, 32, 4, 32), f32)
    for r in range(4):
        for G in range(GROUPS):
            spread[r, 16 + G, r, 4 * G:4 * G + 4] = 1.0
        spread[r, 16, r, 16:] = 1.0
    spread = spread.reshape(128, 128)
    proj_pack = np.concatenate([vrep.T, w_qkv, bias.reshape(128, QKV), one, mq, mk, vrep, np.eye(128, dtype=f32), spread], 1)

    ow = np.zeros((4, 32, D), f32)
    for G in range(GROUPS):
        for r in range(4):
            h = 4 * G + r
            ow[r, 4 * G:4 * G + 4] = t["L0_ffn_o_w"][4 * h:4 * h + 4]
    rank = np.tile(np.arange(E, 0, -1).astype(f32), (128, BATCH))
    const_pack = np.concatenate([
        np.eye(128, dtype=f32), t["L1_cond_k_w"], t["L1_cond_k_w"].T, t["L1_cond_o_w"].T,
        np.tile(t["L1_cond_k_b"], (128, 1)), ow.reshape(128, D),
        t["L0_ffn_router_w"], t["L1_ffn_router_w"].T, np.tile(t["L0_ffn_router_b"], (128, BATCH)), rank,
        t["L0_ffn_b1"].reshape(E * CHUNKS[0], 128).T, t["L0_ffn_b2"].T, t["L0_ffn_o_b"][:, None], t["L1_cond_o_b"][:, None]], 1)
    sel = np.zeros((2, E, E, 128), f32)
    for e in range(E):
        sel[:, e, e] = 1.0
    sel_pack = sel.reshape(16, E * 128)

    def expert_weights(w1, w2, chunks):
        return np.concatenate([w1.transpose(1, 0, 2), w2.reshape(E, chunks, 128, D).transpose(2, 0, 1, 3)
                               .reshape(128, E, chunks * D)], 2)

    arrays = {
        "cond_pack": cond_pack, "proj_pack": proj_pack, "x_t": t["x"].reshape(TOK, D).T,
        "const_pack": const_pack, "sel_pack": sel_pack,
        "w_layer0": expert_weights(t["L0_ffn_w1"], t["L0_ffn_w2"], CHUNKS[0]),
        "w_layer1": expert_weights(t["L1_ffn_w1"], t["L1_ffn_w2"], CHUNKS[1]),
    }
    nc = bacc.Bacc("TRN2", target_bir_lowering=False, num_devices=1)
    feed, args = {}, []
    for name, a in arrays.items():
        a = np.ascontiguousarray(a)
        feed[f"in_{name}"] = a
        args.append(nc.dram_tensor(f"in_{name}", a.shape, mybir.dt.from_np(a.dtype), kind="ExternalInput").ap())
    args.append(nc.dram_tensor("out_t", (D, TOK), F32, kind="ExternalOutput").ap())
    program(nc, *args)
    r = run_bass_kernel_spmd(nc, [feed], core_ids=[0])
    return np.ascontiguousarray(r.results[0]["out_t"].T).reshape(BATCH, SEQ, D)
```
